# Optimizing a Trainium2 kernel written in Bass

```python
import numpy as np
import jax
import jax.numpy as jnp

def _softmax(x, axis=-1):
    return jax.nn.softmax(x, axis=axis)

def _gelu(x):
    return jax.nn.gelu(x, approximate=True)

def _silu(x):
    return jax.nn.silu(x)

def _sigmoid(x):
    return jax.nn.sigmoid(x)

def _layernorm(x, axis=-1, eps=1e-05):
    m = jnp.mean(x, axis=axis, keepdims=True)
    v = jnp.var(x, axis=axis, keepdims=True)
    return (x - m) / jnp.sqrt(v + eps)

def _scatter_add(tgt, idx, src, axis=0):
    return tgt.at[idx].add(src)

def _segment_sum(src, seg, n):
    return jax.ops.segment_sum(src, seg, n)
kernel_name = 'mk_gnn_preln_d4_gnn_r32_9d616a'

def setup_inputs(seed: int=0):
    np.random.seed(seed)
    _w = jnp.asarray

    def _rec_inputs():
        import jax
        import jax.numpy as jnp
        _gk = jax.random.key(seed)
        x = -0.0002117 + 1 * jax.random.normal(jax.random.fold_in(_gk, 1), (3125, 256), jnp.float32)
        src = jax.random.randint(jax.random.fold_in(_gk, 2), (50000,), 0, 3125, jnp.int32)
        dst = jnp.minimum((3125 * jax.random.uniform(jax.random.fold_in(_gk, 3), (50000,)) ** 2.0).astype(jnp.int32), 99999)
        _o = jnp.argsort(dst, stable=True)
        src = src[_o]
        dst = dst[_o]
        edge_attr_32 = 0.000216709 + 1.00012 * jax.random.normal(jax.random.fold_in(_gk, 12), (50000, 32), jnp.float32)
        return (x, src, dst, edge_attr_32)
    x, src, dst, edge_attr_32 = _rec_inputs()

    def _L0_gnn_setup():
        import jax, jax.numpy as jnp
        import numpy as np
        N = 3125
        E = 25000
        EMB = 256
        HID = 256
        EPS = 1e-05

        def _pool_max(h, edge_src, edge_dst):
            pooled = jax.ops.segment_max(h[edge_src], edge_dst, num_segments=N)
            cnt = jax.ops.segment_sum(jnp.ones((edge_dst.shape[0],), h.dtype), edge_dst, num_segments=N)
            return jnp.where((cnt > 0)[:, None], pooled, jnp.zeros((), h.dtype))

        def _layernorm(x, g, b):
            mu = jnp.mean(x, axis=-1, keepdims=True)
            var = jnp.mean(jnp.square(x - mu), axis=-1, keepdims=True)
            return (x - mu) * jax.lax.rsqrt(var + EPS) * g + b
        key = jax.random.key(seed)
        ks = jax.random.split(key, 12)
        s = 0.05
        return {'embeddings': jax.random.normal(ks[0], (N, EMB), jnp.float32), 'edge_src': jax.random.randint(ks[1], (E,), 0, N, jnp.int32), 'edge_dst': jax.random.randint(ks[2], (E,), 0, N, jnp.int32), 'Wp1': jax.random.normal(ks[3], (HID, EMB), jnp.float32) * s, 'bp1': jnp.zeros((HID,), jnp.float32), 'Wm1': jax.random.normal(ks[4], (HID, EMB + HID), jnp.float32) * s, 'bm1': jnp.zeros((HID,), jnp.float32), 'Wm2': jax.random.normal(ks[5], (HID, 2 * HID), jnp.float32) * s, 'bm2': jnp.zeros((HID,), jnp.float32), 'Wm3': jax.random.normal(ks[6], (HID, 2 * HID), jnp.float32) * s, 'bm3': jnp.zeros((HID,), jnp.float32), 'ln2_g': jnp.ones((HID,), jnp.float32), 'ln2_b': jnp.zeros((HID,), jnp.float32), 'ln3_g': jnp.ones((HID,), jnp.float32), 'ln3_b': jnp.zeros((HID,), jnp.float32)}
    _L0_gnn_all = _L0_gnn_setup()
    _L0_gnn_in = {k: v for k, v in _L0_gnn_all.items() if k in ('Wp1', 'bp1', 'Wm1', 'bm1', 'Wm2', 'bm2', 'Wm3', 'bm3', 'ln2_g', 'ln2_b', 'ln3_g', 'ln3_b')}
    del _L0_gnn_all

    def _L1_gnn_setup():
        import jax, jax.numpy as jnp
        import numpy as np
        N = 625
        E = 10000
        IN_F = 256
        HEADS = 4
        OUT_F = 64
        NEG_SLOPE = 0.2

        def _leaky_relu(v):
            return jnp.where(v > 0, v, NEG_SLOPE * v)
        key = jax.random.key(seed)
        k1, k2, k3, k4 = jax.random.split(key, 4)
        x = jax.random.normal(k1, (N, IN_F), dtype=jnp.float32)
        edge_index = jax.random.randint(k2, (2, E), 0, N, dtype=jnp.int64)
        W = jax.random.normal(k3, (IN_F, HEADS * OUT_F), dtype=jnp.float32) * (1.0 / np.sqrt(IN_F))
        att = jax.random.normal(k4, (1, HEADS, 2 * OUT_F), dtype=jnp.float32) * 0.1
        b = jnp.zeros((HEADS * OUT_F,), dtype=jnp.float32)
        return {'x': x, 'W': W, 'att': att, 'b': b, 'edge_index': edge_index}
    _L1_gnn_all = _L1_gnn_setup()
    _L1_gnn_in = {k: v for k, v in _L1_gnn_all.items() if k in ('W', 'att', 'b')}
    del _L1_gnn_all

    def _L2_gnn_setup():
        import jax, jax.numpy as jnp
        import numpy as np
        N, E, D, H, C = (50000, 25000, 256, 4, 64)

        def _gat_layer(h_in, W, a_s, a_d, b, src, dst, n):
            Hh, Cc = a_s.shape
            h = (h_in @ W).reshape(n, Hh, Cc)
            alpha_s = jnp.sum(h * a_s, axis=-1)
            alpha_d = jnp.sum(h * a_d, axis=-1)
            e = jax.nn.leaky_relu(alpha_s[src] + alpha_d[dst], 0.2)
            m = jax.lax.stop_gradient(jax.ops.segment_max(e, dst, num_segments=n))
            ex = jnp.exp(e - m[dst])
            alpha = ex / jax.ops.segment_sum(ex, dst, num_segments=n)[dst]
            out = jax.ops.segment_sum(h[src] * alpha[:, :, None], dst, num_segments=n)
            return out.reshape(n, Hh * Cc) + b
        key = jax.random.key(seed)
        ks = jax.random.split(key, 12)
        x = jax.random.normal(ks[0], (N, D), dtype=jnp.float32)
        src = jax.random.randint(ks[1], (E,), 0, N, dtype=jnp.int32)
        dst = jax.random.randint(ks[2], (E,), 0, N, dtype=jnp.int32)
        dst = jnp.where(dst == src, (dst + 1) % N, dst)
        edge_index = jnp.stack([src, dst], axis=0)
        edge_attr = jax.random.normal(ks[3], (E, 32), dtype=jnp.float32)
        s = 1.0 / np.sqrt(D)
        sc = 1.0 / np.sqrt(C)
        return {'x': x, 'edge_index': edge_index, 'edge_attr': edge_attr, 'W0': jax.random.normal(ks[4], (D, H * C), dtype=jnp.float32) * s, 'a_src0': jax.random.normal(ks[5], (H, C), dtype=jnp.float32) * sc, 'a_dst0': jax.random.normal(ks[6], (H, C), dtype=jnp.float32) * sc, 'b0': jnp.zeros((H * C,), dtype=jnp.float32), 'W1': jax.random.normal(ks[7], (H * C, H * C), dtype=jnp.float32) * s, 'a_src1': jax.random.normal(ks[8], (H, C), dtype=jnp.float32) * sc, 'a_dst1': jax.random.normal(ks[9], (H, C), dtype=jnp.float32) * sc, 'b1': jnp.zeros((H * C,), dtype=jnp.float32)}
    _L2_gnn_all = _L2_gnn_setup()
    _L2_gnn_in = {k: v for k, v in _L2_gnn_all.items() if k in ('W0', 'a_src0', 'a_dst0', 'b0', 'W1', 'a_src1', 'a_dst1', 'b1')}
    del _L2_gnn_all

    def _L3_gnn_setup():
        import jax, jax.numpy as jnp
        import numpy as np
        N_NODES = 3125
        F_DIM = 256
        NNZ = 50000

        def _prelu(x, a):
            return jnp.where(x >= 0, x, a * x)

        def _hconv(x, W, b, src, dst, n):
            xt = x @ W
            ones = jnp.ones(src.shape, xt.dtype)
            D = jax.ops.segment_sum(ones, src, num_segments=n)
            B = jax.ops.segment_sum(ones, dst, num_segments=n)
            Dinv = jnp.where(D > 0, 1.0 / D, 0.0)
            Binv = jnp.where(B > 0, 1.0 / B, 0.0)
            m = jax.ops.segment_sum(xt[src], dst, num_segments=n) * Binv[:, None]
            out = jax.ops.segment_sum(m[dst], src, num_segments=n) * Dinv[:, None]
            return out + b
        key = jax.random.key(seed)
        k0, k1, k2, k3 = jax.random.split(key, 4)
        x = jax.random.normal(k0, (N_NODES, F_DIM), dtype=jnp.float32)
        edge_index = jax.random.randint(k1, (2, NNZ), 0, N_NODES, dtype=jnp.int32)
        scale = (2.0 / F_DIM) ** 0.5
        W1 = jax.random.normal(k2, (F_DIM, F_DIM), dtype=jnp.float32) * scale
        W2 = jax.random.normal(k3, (F_DIM, F_DIM), dtype=jnp.float32) * scale
        b1 = jnp.zeros((F_DIM,), jnp.float32)
        b2 = jnp.zeros((F_DIM,), jnp.float32)
        a = jnp.full((1,), 0.25, jnp.float32)
        return {'x': x, 'edge_index': edge_index, 'W1': W1, 'b1': b1, 'W2': W2, 'b2': b2, 'a': a}
    _L3_gnn_all = _L3_gnn_setup()
    _L3_gnn_in = {k: v for k, v in _L3_gnn_all.items() if k in ('W1', 'b1', 'W2', 'b2', 'a')}
    del _L3_gnn_all
    return {'x': x, 'src': src, 'dst': dst, 'edge_attr_32': edge_attr_32, 'L0_gnn_Wp1': _L0_gnn_in['Wp1'], 'L0_gnn_bp1': _L0_gnn_in['bp1'], 'L0_gnn_Wm1': _L0_gnn_in['Wm1'], 'L0_gnn_bm1': _L0_gnn_in['bm1'], 'L0_gnn_Wm2': _L0_gnn_in['Wm2'], 'L0_gnn_bm2': _L0_gnn_in['bm2'], 'L0_gnn_Wm3': _L0_gnn_in['Wm3'], 'L0_gnn_bm3': _L0_gnn_in['bm3'], 'L0_gnn_ln2_g': _L0_gnn_in['ln2_g'], 'L0_gnn_ln2_b': _L0_gnn_in['ln2_b'], 'L0_gnn_ln3_g': _L0_gnn_in['ln3_g'], 'L0_gnn_ln3_b': _L0_gnn_in['ln3_b'], 'L1_gnn_W': _L1_gnn_in['W'], 'L1_gnn_att': _L1_gnn_in['att'], 'L1_gnn_b': _L1_gnn_in['b'], 'L2_gnn_W0': _L2_gnn_in['W0'], 'L2_gnn_a_src0': _L2_gnn_in['a_src0'], 'L2_gnn_a_dst0': _L2_gnn_in['a_dst0'], 'L2_gnn_b0': _L2_gnn_in['b0'], 'L2_gnn_W1': _L2_gnn_in['W1'], 'L2_gnn_a_src1': _L2_gnn_in['a_src1'], 'L2_gnn_a_dst1': _L2_gnn_in['a_dst1'], 'L2_gnn_b1': _L2_gnn_in['b1'], 'L3_gnn_W1': _L3_gnn_in['W1'], 'L3_gnn_b1': _L3_gnn_in['b1'], 'L3_gnn_W2': _L3_gnn_in['W2'], 'L3_gnn_b2': _L3_gnn_in['b2'], 'L3_gnn_a': _L3_gnn_in['a']}

def reference(x, src, dst, edge_attr_32, L0_gnn_Wp1, L0_gnn_bp1, L0_gnn_Wm1, L0_gnn_bm1, L0_gnn_Wm2, L0_gnn_bm2, L0_gnn_Wm3, L0_gnn_bm3, L0_gnn_ln2_g, L0_gnn_ln2_b, L0_gnn_ln3_g, L0_gnn_ln3_b, L1_gnn_W, L1_gnn_att, L1_gnn_b, L2_gnn_W0, L2_gnn_a_src0, L2_gnn_a_dst0, L2_gnn_b0, L2_gnn_W1, L2_gnn_a_src1, L2_gnn_a_dst1, L2_gnn_b1, L3_gnn_W1, L3_gnn_b1, L3_gnn_W2, L3_gnn_b2, L3_gnn_a):
    import jax
    import jax.numpy as jnp

    def _L0_gnn_ref(embeddings, edge_src, edge_dst, Wp1, bp1, Wm1, bm1, Wm2, bm2, Wm3, bm3, ln2_g, ln2_b, ln3_g, ln3_b):
        import jax, jax.numpy as jnp
        import numpy as np
        N = 3125
        E = 25000
        EMB = 256
        HID = 256
        EPS = 1e-05

        def _pool_max(h, edge_src, edge_dst):
            pooled = jax.ops.segment_max(h[edge_src], edge_dst, num_segments=N)
            cnt = jax.ops.segment_sum(jnp.ones((edge_dst.shape[0],), h.dtype), edge_dst, num_segments=N)
            return jnp.where((cnt > 0)[:, None], pooled, jnp.zeros((), h.dtype))

        def _layernorm(x, g, b):
            mu = jnp.mean(x, axis=-1, keepdims=True)
            var = jnp.mean(jnp.square(x - mu), axis=-1, keepdims=True)
            return (x - mu) * jax.lax.rsqrt(var + EPS) * g + b
        h1 = jax.nn.relu(embeddings @ Wp1.T + bp1)
        p1 = _pool_max(h1, edge_src, edge_dst)
        x = jax.nn.relu(jnp.concatenate([embeddings, p1], axis=1) @ Wm1.T + bm1)
        p2 = _pool_max(x, edge_src, edge_dst)
        y2 = jax.nn.relu(jnp.concatenate([x, p2], axis=1) @ Wm2.T + bm2)
        x = _layernorm(y2 + x, ln2_g, ln2_b)
        p3 = _pool_max(x, edge_src, edge_dst)
        y3 = jax.nn.relu(jnp.concatenate([x, p3], axis=1) @ Wm3.T + bm3)
        x = _layernorm(y3 + x, ln3_g, ln3_b)
        return x

    def _L1_gnn_ref(x, W, att, b, edge_index):
        import jax, jax.numpy as jnp
        import numpy as np
        N = 625
        E = 10000
        IN_F = 256
        HEADS = 4
        OUT_F = 64
        NEG_SLOPE = 0.2

        def _leaky_relu(v):
            return jnp.where(v > 0, v, NEG_SLOPE * v)
        n = x.shape[0]
        heads = att.shape[1]
        d = att.shape[2] // 2
        loops = jnp.arange(n, dtype=edge_index.dtype)
        src = jnp.concatenate([edge_index[0], loops])
        dst = jnp.concatenate([edge_index[1], loops])
        h = (x @ W).reshape(n, heads, d)
        a_src = att[0, :, :d]
        a_dst = att[0, :, d:]
        h_src = h[src]
        scores = jnp.einsum('ehd,hd->eh', _leaky_relu(h_src), a_src) + jnp.einsum('ehd,hd->eh', _leaky_relu(h[dst]), a_dst)
        w = jax.nn.softmax(scores, axis=0)
        out = jax.ops.segment_sum(h_src * w[:, :, None], dst, num_segments=n)
        return out.reshape(n, heads * d) + b

    def _L2_gnn_ref(x, edge_index, edge_attr, W0, a_src0, a_dst0, b0, W1, a_src1, a_dst1, b1):
        import jax, jax.numpy as jnp
        import numpy as np
        N, E, D, H, C = (50000, 25000, 256, 4, 64)

        def _gat_layer(h_in, W, a_s, a_d, b, src, dst, n):
            Hh, Cc = a_s.shape
            h = (h_in @ W).reshape(n, Hh, Cc)
            alpha_s = jnp.sum(h * a_s, axis=-1)
            alpha_d = jnp.sum(h * a_d, axis=-1)
            e = jax.nn.leaky_relu(alpha_s[src] + alpha_d[dst], 0.2)
            m = jax.lax.stop_gradient(jax.ops.segment_max(e, dst, num_segments=n))
            ex = jnp.exp(e - m[dst])
            alpha = ex / jax.ops.segment_sum(ex, dst, num_segments=n)[dst]
            out = jax.ops.segment_sum(h[src] * alpha[:, :, None], dst, num_segments=n)
            return out.reshape(n, Hh * Cc) + b
        n = x.shape[0]
        loops = jnp.arange(n, dtype=edge_index.dtype)
        src = jnp.concatenate([edge_index[0], loops])
        dst = jnp.concatenate([edge_index[1], loops])
        h = jax.nn.gelu(_gat_layer(x, W0, a_src0, a_dst0, b0, src, dst, n), approximate=False)
        h = jax.nn.gelu(_gat_layer(h, W1, a_src1, a_dst1, b1, src, dst, n), approximate=False)
        return h

    def _L3_gnn_ref(x, edge_index, W1, b1, W2, b2, a):
        import jax, jax.numpy as jnp
        import numpy as np
        N_NODES = 3125
        F_DIM = 256
        NNZ = 50000

        def _prelu(x, a):
            return jnp.where(x >= 0, x, a * x)

        def _hconv(x, W, b, src, dst, n):
            xt = x @ W
            ones = jnp.ones(src.shape, xt.dtype)
            D = jax.ops.segment_sum(ones, src, num_segments=n)
            B = jax.ops.segment_sum(ones, dst, num_segments=n)
            Dinv = jnp.where(D > 0, 1.0 / D, 0.0)
            Binv = jnp.where(B > 0, 1.0 / B, 0.0)
            m = jax.ops.segment_sum(xt[src], dst, num_segments=n) * Binv[:, None]
            out = jax.ops.segment_sum(m[dst], src, num_segments=n) * Dinv[:, None]
            return out + b
        src, dst = (edge_index[0], edge_index[1])
        n = x.shape[0]
        h = _prelu(_hconv(x, W1, b1, src, dst, n), a)
        h = _hconv(h, W2, b2, src, dst, n) + x
        return _prelu(h, a)
    edge_index = jnp.stack([src, dst])
    h = jnp.maximum(_layernorm(x, axis=-1), 0.0)
    x = x + _L0_gnn_ref(h, src, dst, L0_gnn_Wp1, L0_gnn_bp1, L0_gnn_Wm1, L0_gnn_bm1, L0_gnn_Wm2, L0_gnn_bm2, L0_gnn_Wm3, L0_gnn_bm3, L0_gnn_ln2_g, L0_gnn_ln2_b, L0_gnn_ln3_g, L0_gnn_ln3_b)
    h = jnp.maximum(_layernorm(x, axis=-1), 0.0)
    x = x + _L1_gnn_ref(h, L1_gnn_W, L1_gnn_att, L1_gnn_b, edge_index)
    h = jnp.maximum(_layernorm(x, axis=-1), 0.0)
    x = x + _L2_gnn_ref(h, edge_index, edge_attr_32, L2_gnn_W0, L2_gnn_a_src0, L2_gnn_a_dst0, L2_gnn_b0, L2_gnn_W1, L2_gnn_a_src1, L2_gnn_a_dst1, L2_gnn_b1)
    h = jnp.maximum(_layernorm(x, axis=-1), 0.0)
    x = x + _L3_gnn_ref(h, edge_index, L3_gnn_W1, L3_gnn_b1, L3_gnn_W2, L3_gnn_b2, L3_gnn_a)
    return x

_drawn_inputs = setup_inputs


def setup_inputs(seed=0):
    import zlib

    import numpy as np

    out = dict(_drawn_inputs(seed))
    spreads = {'L0_gnn_bp1': (0.0, 0.1),
     'L0_gnn_bm1': (0.0, 0.1),
     'L0_gnn_bm2': (0.0, 0.1),
     'L0_gnn_bm3': (0.0, 0.1),
     'L0_gnn_ln2_g': (1.0, 0.2),
     'L0_gnn_ln2_b': (0.0, 0.1),
     'L0_gnn_ln3_g': (1.0, 0.2),
     'L0_gnn_ln3_b': (0.0, 0.1),
     'L1_gnn_b': (0.0, 0.1),
     'L2_gnn_b0': (0.0, 0.331),
     'L2_gnn_b1': (0.0, 0.1),
     'L3_gnn_b1': (0.0, 0.1),
     'L3_gnn_b2': (0.0, 0.1)}
    factors = {'L1_gnn_W': 8.0,
     'L1_gnn_att': 8.0,
     'L2_gnn_a_src0': 8.0,
     'L2_gnn_a_dst0': 75.851,
     'L2_gnn_a_src1': 8.0,
     'L2_gnn_a_dst1': 121.106}
    for name, (base, spread) in spreads.items():
        noise = np.random.default_rng([zlib.crc32(name.encode()), seed]).standard_normal(out[name].shape)
        drawn = base * np.exp(spread * noise) if base else spread * noise
        out[name] = jnp.asarray(drawn.astype(out[name].dtype))
    for name, factor in factors.items():
        out[name] = (out[name] * factor).astype(out[name].dtype)
    return out
```

```python
from contextlib import ExitStack, contextmanager

import concourse.bass as bass
import concourse.mybir as mybir

F32 = mybir.dt.float32
BF16 = mybir.dt.bfloat16
I32 = mybir.dt.int32
ALU = mybir.AluOpType
ACT = mybir.ActivationFunctionType
AX = mybir.AxisListType
DVE = mybir.EngineType.DVE

P = 128
NODES, F = 3125, 256
EDGES = 50000
HEADS = 4
C = F // HEADS
BLOCKS = -(-NODES // P)
ROWS = BLOCKS * P
PAD = ROWS - 1
TILES = 392
CHUNKS = 4
SLOTS = CHUNKS * P * P
STEPS = TILES + BLOCKS - 1
UNROLL = 16
LAG = 4
BIG = float(2.0 ** 126)
FAR = 8192.0
OUTSIDE = 100000.0
W8 = F + HEADS


def build(nc, io, out):
    ctx = ExitStack()
    phases = [0]

    def sb(name, shape, dt=F32):
        return ctx.enter_context(nc.sbuf_tensor(name, shape, dt))

    @contextmanager
    def phase(*names):
        phases[0] += 1
        sems = {n: nc.alloc_semaphore(f"{n}_{phases[0]}") for n in names}
        with nc.Block() as block:
            yield block, sems
        nc.clear_and_free_semaphores(list(sems.values()))
        nc.all_engine_barrier()

    def loop(eng, iterations, step, unroll, drain=0):
        for s in range(unroll):
            step(0, s)
        with eng.Fori(1, iterations) as i:
            for s in range(unroll):
                step(i, s)
        for s in range(drain):
            step(iterations, s)

    def at(i, s, unroll, back=0):
        k = i * unroll + s - back
        return None if isinstance(k, int) and k < 0 else k

    with ctx:
        dst_list = nc.dram_tensor("dst_list", (1 + EDGES + 122 * P,), I32).ap()
        src_list = nc.dram_tensor("src_list", (1 + EDGES + 122 * P,), I32).ap()
        pair_list = nc.dram_tensor("pair_list", (1 + TILES * P + 121 * P, 2), I32).ap()
        table = nc.dram_tensor("table", (ROWS, F), F32).ap()
        ftable = nc.dram_tensor("ftable", (ROWS, HEADS), F32).ap()
        seg_starts = nc.dram_tensor("seg_starts", (SLOTS, 2 * HEADS), F32).ap()
        seg_maxima = nc.dram_tensor("seg_maxima", (SLOTS, HEADS), F32).ap()

        psum = [ctx.enter_context(nc.psum_tensor(f"bank{n}", [P, 512], F32)) for n in range(8)]

        x_res = sb("x_res", [P, BLOCKS * F])
        act_a = sb("act_a", [P, BLOCKS * F])
        act_b = sb("act_b", [P, BLOCKS * F])
        agg = sb("agg", [P, BLOCKS * W8])
        ring = sb("ring", [P, UNROLL * F])
        wrows = sb("wrows", [P, 4 * W8])
        onehot = sb("onehot", [P, 4 * P])
        weights = sb("weights", [P, 4 * F])
        bias_row = sb("bias_row", [1, F])
        row_a = sb("row_a", [P, F])
        row_b = sb("row_b", [P, F])
        ident = sb("ident", [P, P])
        ident_b = sb("ident_b", [P, P], BF16)
        iota_f = sb("iota_f", [P, P])
        iota_b = sb("iota_b", [P, P], BF16)
        iota_p = sb("iota_p", [P, 1])
        ones = sb("ones", [P, P])
        below = sb("below", [P, P])
        tile_no = sb("tile_no", [P, CHUNKS * P])
        step_no = sb("step_no", [P, STEPS])
        of_step = sb("of_step", [P, CHUNKS * STEPS])
        node_d = sb("node_d", [P, STEPS])
        last_d = sb("last_d", [P, STEPS])
        start_d = sb("start_d", [P, STEPS])
        row_d = sb("row_d", [P, STEPS], I32)
        block_d = sb("block_d", [P, STEPS + UNROLL], I32)
        node_s = sb("node_s", [P, STEPS])
        row_s = sb("row_s", [P, STEPS], I32)
        block_s = sb("block_s", [P, STEPS + UNROLL], I32)
        row_t = sb("row_t", [P, CHUNKS * P], I32)
        start_r = sb("start_r", [P, CHUNKS * P])
        deg_d = sb("deg_d", [P, 32])
        deg_s = sb("deg_s", [P, 32])
        first_s = sb("first_s", [P, 32])
        first_row = sb("first_row", [P, BLOCKS], I32)
        final_row = sb("final_row", [P, BLOCKS], I32)
        f_node = sb("f_node", [P, BLOCKS * HEADS])
        gm_node = sb("gm_node", [P, BLOCKS * 2 * HEADS])
        w_self = sb("w_self", [P, BLOCKS * HEADS])
        w_edge = sb("w_edge", [P, STEPS * HEADS])
        slope = sb("slope", [P, 1])
        keep_r = sb("keep_r", [P, CHUNKS * P])
        open_r = sb("open_r", [P, CHUNKS * P])
        chain_keep = sb("chain_keep", [8, CHUNKS * P])
        chain_open = sb("chain_open", [8, CHUNKS * P])
        carry = sb("carry", [8, 1 + CHUNKS * P])
        first_keep = sb("first_keep", [P, CHUNKS])
        first_open = sb("first_open", [P, CHUNKS])
        small = sb("small", [P, 256])
        stage_i = sb("stage_i", [P, UNROLL], I32)
        mark = sb("mark", [P, UNROLL], BF16)
        x_eng = sb("work", [P, 12 * 512])

        def bc(ap, shape):
            return ap.to_broadcast(shape)

        def blocks(t):
            return t[:, 0:BLOCKS * F].rearrange("p (b f) -> p b f", f=F)

        def heads(t):
            return t[:, 0:BLOCKS * F].rearrange("p (b h c) -> p b h c", h=HEADS, c=C)

        agg3 = agg[:, :].rearrange("p (b w) -> p b w", w=W8)
        agg_f = agg3[:, :, 0:F]
        agg_h = agg_f.rearrange("p b (h c) -> p b h c", h=HEADS)
        agg_den = agg3[:, :, F:W8]
        f3 = f_node[:, :].rearrange("p (b h) -> p b h", h=HEADS)
        gm4 = gm_node[:, :].rearrange("p (b g h) -> p b g h", g=2, h=HEADS)
        table_v = table.rearrange("(b p) f -> p b f", p=P)

        def setup():
            with phase("made", "cast", "x_in", "pads", "lists_in") as (block, m):
                made, cast, x_in, pads, lists_in = (m[n] for n in ("made", "cast", "x_in", "pads", "lists_in"))
                pad_i = x_eng[:, 0:256].bitcast(I32)
                first_i = x_eng[:, 256:257].bitcast(I32)

                @block.gpsimd
                def _(g):
                    g.iota(iota_f[:, :], pattern=[[1, P]], base=0, channel_multiplier=0,
                           allow_small_or_imprecise_dtypes=True).then_inc(made, 1)
                    g.iota(iota_p[:, :], pattern=[[0, 1]], base=0, channel_multiplier=1,
                           allow_small_or_imprecise_dtypes=True).then_inc(made, 1)
                    g.iota(tile_no[:, :], pattern=[[P, CHUNKS], [0, P]], base=0, channel_multiplier=1,
                           allow_small_or_imprecise_dtypes=True).then_inc(made, 1)
                    g.iota(step_no[:, :], pattern=[[1, STEPS]], base=0, channel_multiplier=0,
                           allow_small_or_imprecise_dtypes=True).then_inc(made, 1)
                    g.iota(pad_i, pattern=[[0, 256]], base=PAD, channel_multiplier=0).then_inc(made, 1)
                    g.iota(first_i, pattern=[[0, 1]], base=-1, channel_multiplier=0).then_inc(made, 1)

                @block.vector
                def _(v):
                    v.memset(ones[:, :], 1.0).then_inc(cast, 1)
                    v.memset(x_res[:, (BLOCKS - 1) * F:], 0.0).then_inc(pads, 1)
                    v.wait_ge(made, 6)
                    v.tensor_copy(iota_b[:, :], iota_f[:, :]).then_inc(cast, 1)
                    v.tensor_scalar(ident[:, :], iota_f[:, :], iota_p[:, 0:1], None, ALU.is_equal).then_inc(cast, 1)
                    v.tensor_scalar(ident_b[:, :], iota_f[:, :], iota_p[:, 0:1], None, ALU.is_equal).then_inc(cast, 1)
                    v.tensor_scalar(below[:, :], iota_f[:, :], iota_p[:, 0:1], None, ALU.is_gt).then_inc(cast, 1)
                    v.memset(x_eng[:, 512:], 0.0).then_inc(cast, 1)

                @block.sync
                def _(sp):
                    full = (BLOCKS - 1) * P
                    sp.dma_start(blocks(x_res)[:, 0:BLOCKS - 1, :],
                                 io["x"][0:full, :].rearrange("(b p) f -> p b f", p=P)).then_inc(x_in, 16)
                    for name, lst in (("dst", dst_list), ("src", src_list)):
                        sp.dma_start(lst[1:1 + EDGES].rearrange("(a b) -> a b", a=16),
                                     io[name].rearrange("(a b) -> a b", a=16)).then_inc(lists_in, 16)
                    sp.wait_ge(pads, 1)
                    sp.dma_start(x_res[0:NODES - full, (BLOCKS - 1) * F:], io["x"][full:NODES, :]).then_inc(x_in, 16)
                    sp.wait_ge(made, 6)
                    for lst in (dst_list, src_list):
                        sp.dma_start(lst[1 + EDGES:].rearrange("(a b) -> a b", b=P), pad_i[0:122, 0:P]).then_inc(lists_in, 16)
                        sp.dma_start(lst[0:1].rearrange("(a b) -> a b", a=1), first_i[0:1, :]).then_inc(lists_in, 16)
                    pl = pair_list[1 + TILES * P:, :].rearrange("(a b) c -> a (b c)", b=P)
                    sp.dma_start(pl, pad_i[0:121, :]).then_inc(lists_in, 16)
                    sp.dma_start(pair_list[0:1, 0:1], first_i[0:1, :]).then_inc(lists_in, 16)
                    sp.dma_start(pair_list[0:1, 1:2], first_i[0:1, :]).then_inc(lists_in, 16)
                    zero = x_eng[:, 512:512 + 4096]
                    sp.wait_ge(cast, 6)
                    sp.dma_start(seg_starts.rearrange("(p a) c -> p (a c)", p=P), zero).then_inc(lists_in, 16)
                    sp.wait_ge(x_in, 32)
                    sp.wait_ge(lists_in, 16 * 10)

        def row_load(sp, tile, lst, off, sem):
            n = lst.shape[1] if len(lst.shape) > 1 else 1
            if n == 1:
                src = lst[off:off + SLOTS].rearrange("(j t e) -> t j e", j=CHUNKS, t=P)
                sp.dma_start(tile.rearrange("t (j e) -> t j e", j=CHUNKS), src).then_inc(sem, 16)
            else:
                src = lst[off:off + SLOTS, :].rearrange("(j t e) c -> t j (e c)", j=CHUNKS, t=P)
                sp.dma_start(tile.rearrange("t (j e) -> t j e", j=CHUNKS), src).then_inc(sem, 16)

        def walk_tables(by_dst):
            node_k, row_k, block_k = (node_d, row_d, block_d) if by_dst else (node_s, row_s, block_s)
            w = 512 if by_dst else 1024
            raw = [x_eng[:, n * w:(n + 1) * w].bitcast(I32) for n in range(4)]
            if by_dst:
                key_i, prev_i, next_i, pay_i = raw
            else:
                key_i, prev_i, next_i = (r.rearrange("t (s c) -> t s c", c=2)[:, :, 0] for r in raw[0:3])
                pay_i = raw[0].rearrange("t (s c) -> t s c", c=2)[:, :, 1]
            vals = [x_eng[:, 3072 + n * 512:3584 + n * 512] for n in range(5)]
            key_f, prev_f, next_f, pay_f, last_f = vals
            lo_i = small[:, 0:4].bitcast(I32)
            hi_i = small[:, 4:8].bitcast(I32)
            lo = small[:, 8:12]
            hi = small[:, 12:16]
            tno = tile_no[:, :].rearrange("t (j e) -> t j e", e=P)[:, :, 0]
            with phase("loaded", "cast", "ready", "summed", "done") as (block, m):
                loaded, cast, ready, summed, done = (m[n] for n in ("loaded", "cast", "ready", "summed", "done"))

                @block.sync
                def _(sp):
                    if by_dst:
                        row_load(sp, key_i, dst_list, 1, loaded)
                        row_load(sp, prev_i, dst_list, 0, loaded)
                        row_load(sp, next_i, dst_list, 2, loaded)
                        row_load(sp, pay_i, src_list, 1, loaded)
                    else:
                        row_load(sp, raw[0], pair_list, 1, loaded)
                        row_load(sp, raw[1], pair_list, 0, loaded)
                        row_load(sp, raw[2], pair_list, 2, loaded)

                @block.vector
                def _(v):
                    v.memset(block_k[:, 0:LAG], 0).then_inc(done, 1)
                    v.memset(block_k[:, LAG + STEPS:], 0).then_inc(done, 1)
                    v.wait_ge(loaded, 64 if by_dst else 48)
                    for o, i in ((key_f, key_i), (prev_f, prev_i), (next_f, next_i), (pay_f, pay_i)):
                        v.tensor_copy(o, i).then_inc(cast, 1)
                    kk = raw[0].rearrange("t (j e) -> t j e", j=CHUNKS)
                    pp = raw[1].rearrange("t (j e) -> t j e", j=CHUNKS)
                    last_at = (P - 1) * (1 if by_dst else 2)
                    v.tensor_single_scalar(hi_i, kk[:, :, last_at], 7, op=ALU.arith_shift_right).then_inc(cast, 1)
                    v.tensor_single_scalar(lo_i, pp[:, :, 0], 7, op=ALU.arith_shift_right).then_inc(cast, 1)
                    v.wait_ge(cast, 6)
                    v.tensor_tensor(hi, hi_i, tno, ALU.add).then_inc(cast, 1)
                    v.tensor_tensor(lo, lo_i, tno, ALU.add).then_inc(cast, 1)
                    v.wait_ge(cast, 8)
                    for j in range(CHUNKS):
                        v.tensor_scalar(of_step[:, j * STEPS:(j + 1) * STEPS], step_no[:, :], lo[:, j:j + 1], None,
                                        ALU.is_ge).then_inc(cast, 1)
                    v.wait_ge(cast, 12)
                    for j in range(CHUNKS):
                        o = of_step[:, j * STEPS:(j + 1) * STEPS]
                        v.scalar_tensor_tensor(o, step_no[:, :], hi[:, j:j + 1], o, ALU.is_le, ALU.mult).then_inc(ready, 1)
                    if by_dst:
                        v.tensor_tensor(last_f, key_f, next_f, ALU.not_equal).then_inc(cast, 1)
                        v.tensor_tensor(start_r[:, :], key_f, prev_f, ALU.not_equal).then_inc(ready, 1)
                        v.wait_ge(cast, 13)
                        v.scalar_tensor_tensor(last_f, key_f, FAR, last_f, ALU.add, ALU.mult).then_inc(cast, 1)
                        v.wait_ge(cast, 14)
                        v.tensor_scalar(last_f, last_f, -FAR, None, ALU.add).then_inc(ready, 1)
                    v.wait_ge(summed, 1)
                    blk = x_eng[:, 0:STEPS]
                    v.tensor_tensor(blk, step_no[:, :], psum[0][:, 0:STEPS], ALU.subtract).then_inc(done, 1)
                    v.wait_ge(done, 3)
                    v.tensor_copy(block_k[:, LAG:LAG + STEPS], blk).then_inc(done, 1)
                    v.tensor_copy(row_k[:, :], psum[2][:, 0:STEPS]).then_inc(done, 1)
                    v.scalar_tensor_tensor(node_k[:, :], blk, -float(P), psum[1][:, 0:STEPS], ALU.mult, ALU.add).then_inc(done, 1)
                    if by_dst:
                        v.scalar_tensor_tensor(last_d[:, :], blk, -float(P), psum[3][:, 0:STEPS], ALU.mult, ALU.add).then_inc(done, 1)
                        v.tensor_scalar(start_d[:, :], psum[4][:, 0:STEPS], -BIG, None, ALU.mult).then_inc(done, 1)
                        v.tensor_copy(row_t[:, :], psum[5][:, :]).then_inc(done, 1)

                @block.tensor
                def _(pe):
                    pe.wait_ge(ready, 6 if by_dst else 4)
                    rows = [tile_no[:, :], key_f, pay_f] + ([last_f, start_r[:, :]] if by_dst else [])
                    for n, r in enumerate(rows):
                        for j in range(CHUNKS):
                            last = pe.matmul(psum[n][:, 0:STEPS], r[:, j * P:(j + 1) * P], of_step[:, j * STEPS:(j + 1) * STEPS],
                                             start=(j == 0), stop=(j == CHUNKS - 1))
                    if by_dst:
                        for j in range(CHUNKS):
                            last = pe.transpose(psum[5][:, j * P:(j + 1) * P], pay_f[:, j * P:(j + 1) * P], ident[:, :])
                    last.then_inc(summed, 1)

        U8 = 8
        lo_key = [x_eng[:, 0:512], x_eng[:, 512:1024]]
        hi_key = [x_eng[:, 1024:1536], x_eng[:, 1536:2048]]
        pos = x_eng[:, 2048:2560]

        def split_keys():
            raw = [x_eng[:, 2048 + n * 512:2560 + n * 512].bitcast(I32) for n in range(2)]
            part = [x_eng[:, 3072 + n * 512:3584 + n * 512].bitcast(I32) for n in range(4)]
            val = [x_eng[:, 5120:5632], x_eng[:, 5632:6144]]
            with phase("loaded", "cast", "turned", "done") as (block, m):
                loaded, cast, turned, done = (m[n] for n in ("loaded", "cast", "turned", "done"))

                @block.sync
                def _(sp):
                    row_load(sp, raw[0], dst_list, 1, loaded)
                    row_load(sp, raw[1], src_list, 1, loaded)

                @block.vector
                def _(v):
                    v.wait_ge(loaded, 32)
                    for n in range(2):
                        v.tensor_single_scalar(part[2 * n], raw[n], 127, op=ALU.bitwise_and).then_inc(cast, 1)
                        v.tensor_single_scalar(part[2 * n + 1], raw[n], 7, op=ALU.arith_shift_right).then_inc(cast, 1)
                    for n in range(4):
                        v.wait_ge(cast, 4 + n)
                        if n >= 2:
                            v.wait_ge(turned, n - 1)
                        v.tensor_copy(val[n % 2], part[n]).then_inc(cast, 1)
                    for n, o in enumerate((lo_key[0], hi_key[0], lo_key[1], hi_key[1])):
                        v.wait_ge(turned, n + 1)
                        v.tensor_copy(o, psum[n][:, :]).then_inc(done, 1)

                @block.tensor
                def _(pe):
                    for n in range(4):
                        pe.wait_ge(cast, 5 + n)
                        for j in range(CHUNKS):
                            last = pe.transpose(psum[n][:, j * P:(j + 1) * P], val[n % 2][:, j * P:(j + 1) * P], ident[:, :])
                        last.then_inc(turned, 1)

        def count():
            oh = ring[:, 0:2048].bitcast(BF16)
            def ohl(s, n):
                return oh[:, (s * 2 + n) * 160:(s * 2 + n) * 160 + P]
            def ohh(s, n):
                return oh[:, (s * 2 + n) * 160 + P:(s * 2 + n + 1) * 160]
            with phase("made", "counted", "copied", "totals", "done") as (block, m):
                made, counted, copied, totals, done = (m[n] for n in ("made", "counted", "copied", "totals", "done"))

                @block.vector
                def _(v):
                    def step(i, s):
                        t = i * U8 + s
                        if s == 0 and not isinstance(i, int):
                            v.wait_ge(counted, i * U8)
                        for n in range(2):
                            v.tensor_scalar(ohl(s, n), iota_b[:, :], lo_key[n][:, bass.ds(t, 1)], None, ALU.is_equal)
                            last = v.tensor_scalar(ohh(s, n), iota_b[:, 0:32], hi_key[n][:, bass.ds(t, 1)], None, ALU.is_equal)
                        last.then_inc(made, 1)
                    loop(v, TILES // U8, step, U8)
                    v.wait_ge(counted, TILES)
                    v.tensor_copy(deg_d[:, :], psum[0][:, 0:32]).then_inc(copied, 1)
                    v.tensor_copy(deg_s[:, :], psum[1][:, 0:32]).then_inc(copied, 1)
                    v.wait_ge(totals, 1)
                    tot = small[:, 0:64]
                    inc = small[:, 64:128]
                    pos_ = small[:, 128:160]
                    fst = small[:, 160:192]
                    fin = small[:, 192:224]
                    v.tensor_copy(tot[:, 0:32], psum[2][:, 0:32]).then_inc(done, 1)
                    v.tensor_copy(tot[:, 32:64], psum[2][:, 32:64]).then_inc(done, 1)
                    v.wait_ge(done, 2)
                    for n in range(2):
                        v.tensor_tensor_scan(inc[:, 32 * n:32 * n + 32], ones[:, 0:32], tot[:, 32 * n:32 * n + 32], 0.0,
                                             ALU.mult, ALU.add).then_inc(done, 1)
                    v.wait_ge(done, 4)
                    v.tensor_tensor(inc, inc, tot, ALU.subtract).then_inc(done, 1)
                    v.wait_ge(done, 5)
                    v.tensor_tensor(fst, inc[:, 0:32], psum[3][:, 0:32], ALU.add).then_inc(done, 1)
                    v.tensor_tensor(first_s[:, :], inc[:, 32:64], psum[3][:, 32:64], ALU.add).then_inc(done, 1)
                    v.tensor_scalar(pos_, deg_d[:, :], 0.0, None, ALU.is_gt).then_inc(done, 1)
                    v.wait_ge(done, 8)
                    v.scalar_tensor_tensor(fin, fst, -1.0 - OUTSIDE, deg_d[:, :], ALU.add, ALU.add).then_inc(done, 1)
                    v.wait_ge(done, 9)
                    v.tensor_tensor(fin, fin, pos_, ALU.mult).then_inc(done, 1)
                    v.scalar_tensor_tensor(fst, fst, -OUTSIDE, pos_, ALU.add, ALU.mult).then_inc(done, 1)
                    v.wait_ge(done, 11)
                    v.tensor_scalar(first_row[:, :], fst[:, 0:BLOCKS], OUTSIDE, None, ALU.add).then_inc(done, 1)
                    v.tensor_scalar(final_row[:, :], fin[:, 0:BLOCKS], OUTSIDE, None, ALU.add).then_inc(done, 1)

                @block.tensor
                def _(pe):
                    def step(i, s):
                        first = isinstance(i, int) and s == 0
                        pe.wait_ge(made, i * U8 + s + 1)
                        for n in range(2):
                            last = pe.matmul(psum[n][:, 0:32], ohl(s, n), ohh(s, n), start=first, stop=False,
                                             skip_group_check=True)
                        last.then_inc(counted, 1)
                    loop(pe, TILES // U8, step, U8)
                    pe.wait_ge(copied, 2)
                    for w, bank in ((ones, psum[2]), (below, psum[3])):
                        pe.matmul(bank[:, 0:32], w[:, :], deg_d[:, :], start=True, stop=True)
                        last = pe.matmul(bank[:, 32:64], w[:, :], deg_s[:, :], start=True, stop=True)
                    last.then_inc(totals, 1)

        def places():
            oh = ring[:, 0:2048].bitcast(BF16)
            low = lambda s: oh[:, s * P:(s + 1) * P]
            high = lambda s: oh[:, 1024 + s * 32:1024 + (s + 1) * 32]
            lowt_b = lambda s: oh[:, 1280 + (s % 4) * P:1280 + (s % 4 + 1) * P]
            same = lambda s: oh[:, 1792 + (s % 4) * P:1792 + (s % 4 + 1) * P]
            lowt = lambda s: ring[:, 2048 + (s % 4) * P:2048 + (s % 4 + 1) * P]
            seen = lambda s: ring[:, 2560 + (s % 4) * 32:2560 + (s % 4 + 1) * 32]
            junk = lambda s: ring[:, 2688 + (s % U8) * 32:2720 + (s % U8) * 32]
            turn = [psum[n][:, :].bitcast(BF16) for n in (0, 1)]
            with phase("made", "turned", "lifted", "running", "snapped", "paired", "masked", "looked", "placed", "cast") as (block, m):
                made, turned, lifted, running, snapped = (m[n] for n in ("made", "turned", "lifted", "running", "snapped"))
                paired, masked, looked, placed, cast = (m[n] for n in ("paired", "masked", "looked", "placed", "cast"))

                @block.vector
                def _(v):
                    def step(i, s):
                        t = at(i, s, U8)
                        if at(i, s, U8, U8) is not None:
                            v.wait_ge(looked, at(i, s, U8, U8) + 1)
                        if at(i, s, U8, U8) is not None:
                            v.wait_ge(placed, at(i, s, U8, U8) + 1)
                        if not (isinstance(t, int) and t >= TILES):
                            v.tensor_scalar(low(s), iota_b[:, :], lo_key[1][:, bass.ds(t, 1)], None, ALU.is_equal)
                            v.tensor_scalar(high(s), iota_b[:, 0:32], hi_key[1][:, bass.ds(t, 1)], None, ALU.is_equal).then_inc(made, 1)
                        b = at(i, s, U8, 1)
                        if b is not None and not (isinstance(b, int) and b >= TILES):
                            v.wait_ge(paired, b + 1)
                            if at(i, s, U8, 5) is not None:
                                v.wait_ge(looked, at(i, s, U8, 5) + 1)
                            v.tensor_tensor(same(s - 1), psum[2 + (s - 1) % 2][:, 0:P], below[:, :], ALU.mult).then_inc(masked, 1)
                        c = at(i, s, U8, 2)
                        if c is not None:
                            v.wait_ge(looked, c + 1)
                            v.scalar_tensor_tensor(junk(s - 2), psum[4 + (s - 2) % 2][:, 0:32], 1.0, high((s - 2) % U8),
                                                   ALU.mult, ALU.mult, accum_out=pos[:, bass.ds(c, 1)]).then_inc(placed, 1)
                    loop(v, TILES // U8, step, U8, drain=2)
                    v.wait_ge(placed, TILES)

                @block.scalar
                def _(act):
                    def step(i, s):
                        t = at(i, s, U8)
                        act.wait_ge(turned, t + 1)
                        if at(i, s, U8, 4) is not None:
                            act.wait_ge(looked, at(i, s, U8, 4) + 1)
                        nc.scalar.copy(lowt_b(s), turn[s % 2][:, 0:P]).then_inc(lifted, 1)
                        nc.scalar.copy(lowt(s), turn[s % 2][:, 0:P]).then_inc(lifted, 1)
                        act.wait_ge(running, t + 1)
                        nc.scalar.copy(seen(s), psum[6][:, 0:32]).then_inc(snapped, 1)
                    loop(act, TILES // U8, step, U8)

                @block.tensor
                def _(pe):
                    pe.matmul(psum[6][:, 0:32], ident[:, :], first_s[:, :], start=True, stop=False,
                              skip_group_check=True).then_inc(running, 1)
                    def step(i, s):
                        t = at(i, s, U8)
                        if not (isinstance(t, int) and t >= TILES):
                            pe.wait_ge(made, t + 1)
                            if at(i, s, U8, 2) is not None:
                                pe.wait_ge(lifted, 2 * at(i, s, U8, 2) + 2)
                            pe.transpose(turn[s % 2][:, 0:P], low(s), ident_b[:, :]).then_inc(turned, 1)
                            pe.wait_ge(snapped, t + 1)
                            pe.matmul(psum[6][:, 0:32], low(s), high(s), start=False, stop=False,
                                      skip_group_check=True).then_inc(running, 1)
                            pe.wait_ge(lifted, 2 * t + 2)
                            if at(i, s, U8, 2) is not None:
                                pe.wait_ge(masked, at(i, s, U8, 2) + 1)
                            pe.matmul(psum[2 + s % 2][:, 0:P], lowt_b(s), lowt_b(s), start=True, stop=True).then_inc(paired, 1)
                        b = at(i, s, U8, 1)
                        if b is not None:
                            pe.wait_ge(masked, b + 1)
                            if at(i, s, U8, 3) is not None:
                                pe.wait_ge(placed, at(i, s, U8, 3) + 1)
                            o = psum[4 + (s - 1) % 2][:, 0:32]
                            pe.matmul(o, lowt(s - 1), seen(s - 1), start=True, stop=False)
                            pe.matmul(o, same(s - 1), high((s - 1) % U8), start=False, stop=True).then_inc(looked, 1)
                    loop(pe, TILES // U8, step, U8, drain=1)

        def scatter_pairs():
            pair = x_eng[:, 2560:2560 + 1024].bitcast(I32)
            pos_i = x_eng[:, 3584:4096].bitcast(I32)
            tmp = x_eng[:, 4096:4608]
            pair3 = pair.rearrange("p (t c) -> p t c", c=2)
            sp_i = [ring[:, h * 8:h * 8 + 8].bitcast(I32) for h in range(2)]
            sp_p = [ring[:, 32 + h * 16:48 + h * 16].bitcast(I32) for h in range(2)]
            with phase("cast", "ready", "staged", "turn_go", "sent0", "sent1", "done") as (block, m):
                cast, ready, staged, turn_go, done = (m[n] for n in ("cast", "ready", "staged", "turn_go", "done"))
                sent = [m["sent0"], m["sent1"]]

                @block.vector
                def _(v):
                    v.tensor_scalar(pos_i[:, 0:TILES], pos[:, 0:TILES], 1.0, None, ALU.add).then_inc(cast, 1)
                    for n, c in ((1, 0), (0, 1)):
                        v.scalar_tensor_tensor(pair3[:, 0:TILES, c], hi_key[n][:, 0:TILES], float(P), lo_key[n][:, 0:TILES],
                                               ALU.mult, ALU.add).then_inc(cast, 1)
                    v.wait_ge(cast, 3)
                    v.sem_inc(ready, 1)

                @block.gpsimd
                def _(g):
                    g.wait_ge(ready, 1)
                    def half(i, h):
                        t = i * 16 + h * 8
                        if not isinstance(i, int):
                            g.wait_ge(sent[h], i * 128)
                            g.sem_inc(turn_go, 1)
                        elif i > 0:
                            g.wait_ge(sent[h], i * 128)
                        g.tensor_copy(sp_i[h], pos_i[:, bass.ds(t, 8)]).then_inc(staged, 1)
                        g.tensor_copy(sp_p[h], pair[:, bass.ds(t * 2, 16)]).then_inc(staged, 1)
                        g.wait_ge(staged, i * 4 + h * 2 + 2)
                        g.sem_inc(turn_go, 1)
                        for n in range(8):
                            g.indirect_dma_start(out=pair_list[:, :],
                                                 out_offset=bass.IndirectOffsetOnAxis(ap=sp_i[h][:, n:n + 1], axis=0),
                                                 in_=sp_p[h][:, 2 * n:2 * n + 2], in_offset=None).then_inc(sent[h], 16)
                    half(0, 0)
                    half(0, 1)
                    with g.Fori(1, 24) as i:
                        half(i, 0)
                        half(i, 1)
                    half(24, 0)
                    g.wait_ge(sent[0], 25 * 128)
                    g.wait_ge(sent[1], 24 * 128)

        def store_table(src_tile, with_ftable=False):
            with phase("stored") as (block, m):
                @block.sync
                def _(sp):
                    sp.dma_start(table_v, blocks(src_tile)).then_inc(m["stored"], 16)
                    sp.wait_ge(m["stored"], 16)

        def layernorm(src, dst, affine=None, add_to=None):
            s3, d3 = blocks(src), blocks(dst)
            mean, var, rstd = small[:, 0:BLOCKS], small[:, 32:32 + BLOCKS], small[:, 64:64 + BLOCKS]
            shape = [P, BLOCKS, F]
            sq = agg_f
            with phase("rows_in", "vec", "sc") as (block, m):
                rows_in, vec, sc = (m[n] for n in ("rows_in", "vec", "sc"))

                @block.sync
                def _(sp):
                    if affine:
                        sp.dma_start(row_a[:, :], bc(io[affine[0]].rearrange("(o f) -> o f", o=1), [P, F])).then_inc(rows_in, 16)
                        sp.dma_start(row_b[:, :], bc(io[affine[1]].rearrange("(o f) -> o f", o=1), [P, F])).then_inc(rows_in, 16)

                @block.vector
                def _(v):
                    n = 0
                    def done(inst):
                        inst.then_inc(vec, 1)
                    done(v.tensor_reduce(mean, s3, AX.X, ALU.add))
                    v.wait_ge(vec, 1)
                    done(v.tensor_scalar(mean, mean, 1.0 / F, None, ALU.mult))
                    v.wait_ge(vec, 2)
                    done(v.tensor_tensor(d3, s3, bc(mean.unsqueeze(2), shape), ALU.subtract))
                    v.wait_ge(sc, 1)
                    done(v.tensor_reduce(var, sq, AX.X, ALU.add))
                    v.wait_ge(vec, 4)
                    done(v.tensor_scalar(var, var, 1.0 / F, 1e-5, ALU.mult, ALU.add))
                    v.wait_ge(sc, 2)
                    done(v.reciprocal(rstd, rstd))
                    v.wait_ge(vec, 6)
                    done(v.tensor_tensor(d3, d3, bc(rstd.unsqueeze(2), shape), ALU.mult))
                    if affine:
                        v.wait_ge(rows_in, 32)
                        v.wait_ge(vec, 7)
                        done(v.tensor_tensor(d3, d3, bc(row_a[:, :].unsqueeze(1), shape), ALU.mult))
                        v.wait_ge(vec, 8)
                        done(v.tensor_tensor(d3, d3, bc(row_b[:, :].unsqueeze(1), shape), ALU.add))
                        if add_to is not None:
                            v.wait_ge(vec, 9)
                            done(v.tensor_tensor(blocks(add_to), blocks(add_to), d3, ALU.add))

                @block.scalar
                def _(act):
                    act.wait_ge(vec, 3)
                    nc.scalar.activation(sq, d3, ACT.Square).then_inc(sc, 1)
                    act.wait_ge(vec, 5)
                    nc.scalar.activation(rstd, var, ACT.Sqrt).then_inc(sc, 1)
                    if not affine:
                        act.wait_ge(vec, 7)
                        nc.scalar.activation(dst[:, :], dst[:, :], ACT.Relu).then_inc(sc, 1)

        def load_weights(name, turned):
            w = io[name]
            ins = w.shape[1] if turned else w.shape[0]
            n = ins // P
            raw = x_eng[:, 0:2 * ins]
            with phase("w_in", "turned", "copied") as (block, m):
                w_in, turned_s, copied = m["w_in"], m["turned"], m["copied"]

                @block.sync
                def _(sp):
                    if turned:
                        sp.dma_start(raw.rearrange("p (o i) -> p o i", o=2), w.rearrange("(o p) i -> p o i", p=P)).then_inc(w_in, 16)
                    else:
                        sp.dma_start(weights[:, 0:n * F].rearrange("p (c o) -> p c o", c=n),
                                     w.rearrange("(c p) o -> p c o", p=P)).then_inc(w_in, 16)
                    sp.wait_ge(w_in, 16)

                if turned:
                    @block.tensor
                    def _(pe):
                        pe.wait_ge(w_in, 16)
                        for c in range(n):
                            for o in range(2):
                                last = pe.transpose(psum[c][:, o * P:(o + 1) * P], raw[:, o * ins + c * P:o * ins + (c + 1) * P],
                                                    ident[:, :])
                            last.then_inc(turned_s, 1)

                    @block.vector
                    def _(v):
                        for c in range(n):
                            v.wait_ge(turned_s, c + 1)
                            v.tensor_copy(weights[:, c * F:(c + 1) * F], psum[c][:, 0:F]).then_inc(copied, 1)

        def linear(inputs, dst, bias=None, relu=False, plus=None, to_table=False):
            U = 5
            n = 2 * len(inputs)
            stage = lambda s: x_eng[:, s * n * P:(s + 1) * n * P]
            lhs = lambda s: x_eng[:, (5 + s) * n * P:(6 + s) * n * P] if n == 2 else ring[:, s * n * P:(s + 1) * n * P]
            res = lambda s: psum[s][:, 0:F]
            tab5 = table.rearrange("(g b p) f -> g p b f", b=U, p=P)
            with phase("row_in", "staged", "go", "turned", "copied", "multiplied", "finished", "stored") as (block, m):
                row_in, staged, go, turned = (m[x] for x in ("row_in", "staged", "go", "turned"))
                copied, multiplied, finished, stored = (m[x] for x in ("copied", "multiplied", "finished", "stored"))

                @block.scalar
                def _(act):
                    def step(i, s):
                        for c, t in enumerate(inputs):
                            if isinstance(i, int):
                                if i > 0:
                                    act.wait_ge(turned, (i - 1) * U + s + 1)
                            elif c == 0:
                                act.wait_ge(turned, (i - 1) * U + s + 1)
                                act.sem_inc(go, 1)
                            stride = W8 if t is agg else F
                            last = nc.scalar.copy(stage(s)[:, c * F:(c + 1) * F], t[:, bass.ds((i * U + s) * stride, F)])
                        last.then_inc(staged, 1)
                    loop(act, BLOCKS // U, step, U)

                @block.tensor
                def _(pe):
                    if bias:
                        pe.wait_ge(row_in, 16)
                    def step(i, s):
                        b = i * U + s
                        if not (isinstance(b, int) and b >= BLOCKS):
                            pe.wait_ge(staged, b + 1)
                            if not isinstance(i, int):
                                pe.wait_ge(finished, (i - 1) * U + s + 1)
                            for c in range(n):
                                last = pe.transpose(psum[s][:, c * P:(c + 1) * P], stage(s)[:, c * P:(c + 1) * P], ident[:, :])
                            last.then_inc(turned, 1)
                        q = at(i, s, U, 1)
                        if q is not None:
                            r = (s - 1) % U
                            pe.wait_ge(copied, q + 1)
                            for c in range(n):
                                last = pe.matmul(res(r), lhs(r)[:, c * P:(c + 1) * P], weights[:, c * F:(c + 1) * F],
                                                 start=(c == 0), stop=(c == n - 1 and not bias))
                            if bias:
                                last = pe.matmul(res(r), ones[0:1, :], bias_row[0:1, :], start=False, stop=True)
                            last.then_inc(multiplied, 1)
                    loop(pe, BLOCKS // U, step, U, drain=1)

                @block.vector
                def _(v):
                    def step(i, s):
                        b = i * U + s
                        if not (isinstance(b, int) and b >= BLOCKS):
                            v.wait_ge(turned, b + 1)
                            if not isinstance(i, int):
                                v.wait_ge(multiplied, (i - 1) * U + s + 1)
                            v.tensor_copy(lhs(s), psum[s][:, 0:n * P]).then_inc(copied, 1)
                        q = at(i, s, U, 2)
                        if q is not None:
                            r = (s - 2) % U
                            v.wait_ge(multiplied, q + 1)
                            o = dst[:, bass.ds(q * F, F)]
                            if plus is not None:
                                v.scalar_tensor_tensor(o, res(r), 0.0, plus[:, bass.ds(q * F, F)], ALU.max, ALU.add).then_inc(finished, 1)
                            elif relu:
                                v.tensor_scalar(o, res(r), 0.0, None, ALU.max).then_inc(finished, 1)
                            else:
                                v.tensor_copy(o, res(r)).then_inc(finished, 1)
                    loop(v, BLOCKS // U, step, U, drain=2)

                @block.sync
                def _(sp):
                    if bias:
                        sp.dma_start(bias_row[:, :], io[bias].rearrange("(o f) -> o f", o=1)).then_inc(row_in, 16)
                        sp.wait_ge(row_in, 16)
                    if to_table:
                        for g in range(BLOCKS // U):
                            sp.wait_ge(finished, (g + 1) * U)
                            sp.dma_start(tab5[g], blocks(dst)[:, g * U:(g + 1) * U, :]).then_inc(stored, 16)
                        sp.wait_ge(stored, 16 * (BLOCKS // U))

        def gathers(g, rows, src, dest, m, steps, freed, unroll=UNROLL):
            half = unroll // 2
            def eight(i, h):
                if not isinstance(i, int):
                    g.wait_ge(freed, i * unroll + h * half - half)
                    g.sem_inc(m["go"], 1)
                g.tensor_copy(stage_i[:, h * half:(h + 1) * half], rows[:, bass.ds(i * unroll + h * half, half)]).then_inc(m["staged"], 1)
                g.wait_ge(m["staged"], i * 2 + h + 1)
                g.sem_inc(m["go"], 1)
                for n in range(h * half, (h + 1) * half):
                    g.indirect_dma_start(out=dest(n), out_offset=None, in_=src,
                                         in_offset=bass.IndirectOffsetOnAxis(ap=stage_i[:, n:n + 1], axis=0)).then_inc(m[f"row{n}"], 16)
            eight(0, 0)
            eight(0, 1)
            with g.Fori(1, steps // unroll) as i:
                eight(i, 0)
                eight(i, 1)

        ROW_SEMS = [f"row{n}" for n in range(UNROLL)]
        slot = lambda s: ring[:, (s % UNROLL) * F:(s % UNROLL + 1) * F]
        oneh = lambda s: onehot[:, (s % 4) * P:(s % 4 + 1) * P]

        def add_to_block(v, m, block_tab, i, s, blk, width, lag):
            q = at(i, s, UNROLL, lag)
            if q is None:
                return
            v.wait_ge(m["brought"], q + 1)
            v.wait_ge(m["added"], q + 1)
            o = agg[:, bass.ds(blk * W8, width)]
            v.tensor_tensor(o, o, psum[(s - lag) % 4][:, 0:width], ALU.add).then_inc(m["added"], 1)

        def load_blocks(v, block_tab, i, lag):
            _, vals = nc.values_load_multi_w_load_instructions(
                block_tab[0:1, bass.ds(i * UNROLL + LAG - lag, UNROLL)], engines=(DVE,), min_val=0, max_val=BLOCKS - 1,
                skip_runtime_bounds_check_because="counted from the steps")
            return vals

        def block_loop(v, block_tab, lag, step):
            vals = load_blocks(v, block_tab, 0, lag)
            for s in range(UNROLL):
                step(0, s, vals[s])
            with v.Fori(1, STEPS // UNROLL) as i:
                vals = load_blocks(v, block_tab, i, lag)
                for s in range(UNROLL):
                    step(i, s, vals[s])
            n = STEPS // UNROLL
            vals = load_blocks(v, block_tab, n, lag)
            for s in range(lag):
                step(n, s, vals[s])

        def sum_pass(by_dst, weighted):
            node_k, row_k, block_k = (node_d, row_d, block_d) if by_dst else (node_s, row_s, block_s)
            width = W8 if weighted else F
            lag = LAG
            wrow = lambda s: wrows[:, (s % 4) * W8:(s % 4 + 1) * W8]
            with phase("freed", "go", "staged", "made", "weighed", "brought", "added", *ROW_SEMS) as (block, m):

                @block.gpsimd
                def _(g):
                    gathers(g, row_k, table[:, :], slot, m, STEPS, m["freed"] if weighted else m["brought"])

                @block.vector
                def _(v):
                    v.memset(agg[:, :], 0.0).then_inc(m["added"], 1)
                    def step(i, s, blk):
                        k = i * UNROLL + s
                        if not (isinstance(k, int) and k >= STEPS):
                            if at(i, s, UNROLL, 4) is not None:
                                v.wait_ge(m["brought"], at(i, s, UNROLL, 4) + 1)
                            v.tensor_scalar(oneh(s), iota_f[:, :], node_k[:, bass.ds(k, 1)], None, ALU.is_equal).then_inc(m["made"], 1)
                            if weighted:
                                w4 = w_edge[:, bass.ds(k * HEADS, HEADS)]
                                v.wait_ge(m[f"row{s}"], i * 16 + 16)
                                v.tensor_tensor(wrow(s)[:, 0:F].rearrange("p (h c) -> p h c", h=HEADS),
                                                slot(s).rearrange("p (h c) -> p h c", h=HEADS),
                                                bc(w4.unsqueeze(2), [P, HEADS, C]), ALU.mult).then_inc(m["freed"], 1)
                                v.tensor_copy(wrow(s)[:, F:W8], w4).then_inc(m["weighed"], 1)
                        add_to_block(v, m, block_k, i, s, blk, width, lag)
                    block_loop(v, block_k, lag, step)

                @block.tensor
                def _(pe):
                    def step(i, s):
                        k = i * UNROLL + s
                        pe.wait_ge(m["made"], k + 1)
                        if at(i, s, UNROLL, 4) is not None:
                            pe.wait_ge(m["added"], at(i, s, UNROLL, 4) + 2)
                        if weighted:
                            pe.wait_ge(m["freed"], k + 1)
                            pe.wait_ge(m["weighed"], k + 1)
                            pe.matmul(psum[s % 4][:, 0:W8], oneh(s), wrow(s), start=True, stop=True).then_inc(m["brought"], 1)
                        else:
                            pe.wait_ge(m[f"row{s}"], i * 16 + 16)
                            pe.matmul(psum[s % 4][:, 0:F], oneh(s), slot(s), start=True, stop=True).then_inc(m["brought"], 1)
                    loop(pe, STEPS // UNROLL, step, UNROLL)

        def max_pass():
            lag = LAG
            run = lambda s, h: wrows[:, (s % 2) * F + h * P:(s % 2) * F + (h + 1) * P]
            back = lambda s: wrows[:, 512 + (s % 2) * F:768 + (s % 2) * F]
            mask = lambda s: small[:, (s % 2) * P:(s % 2 + 1) * P]
            tg = lambda s: psum[4 + s % 2]
            tb = lambda s: psum[6 + s % 2]
            with phase("go", "staged", "marked", "made", "turned", "masked", "scanned", "returned", "lifted",
                       "brought", "added", *ROW_SEMS) as (block, m):

                @block.gpsimd
                def _(g):
                    gathers(g, row_d, table[:, :], slot, m, STEPS, m["turned"])

                @block.tensor
                def _(pe):
                    def step(i, s):
                        k = i * UNROLL + s
                        if not (isinstance(k, int) and k >= STEPS):
                            if s == 0:
                                pe.wait_ge(m["marked"], i + 1)
                            pe.wait_ge(m[f"row{s}"], i * 16 + 16)
                            if at(i, s, UNROLL, 2) is not None:
                                pe.wait_ge(m["scanned"], 2 * at(i, s, UNROLL, 2) + 2)
                            for h in range(2):
                                pe.transpose(tg(s)[:, h * P:(h + 1) * P], slot(s)[:, h * P:(h + 1) * P], ident[:, :])
                            pe.matmul(tg(s)[:, F:F + P], bc(mark[:, s:s + 1], [P, P]), ident_b[:, :], start=True, stop=True,
                                      skip_group_check=True).then_inc(m["turned"], 1)
                        q = at(i, s, UNROLL, 1)
                        if q is not None and not (isinstance(q, int) and q >= STEPS):
                            pe.wait_ge(m["scanned"], 2 * q + 2)
                            if at(i, s, UNROLL, 3) is not None:
                                pe.wait_ge(m["lifted"], at(i, s, UNROLL, 3) + 1)
                            for h in range(2):
                                last = pe.transpose(tb(s - 1)[:, h * P:(h + 1) * P], run(s - 1, h), ident[:, :])
                            last.then_inc(m["returned"], 1)
                        q = at(i, s, UNROLL, 2)
                        if q is not None:
                            pe.wait_ge(m["made"], q + 1)
                            pe.wait_ge(m["lifted"], q + 1)
                            if at(i, s, UNROLL, 6) is not None:
                                pe.wait_ge(m["added"], at(i, s, UNROLL, 6) + 3)
                            pe.matmul(psum[(s - 2) % 4][:, 0:F], oneh(s - 2), back(s - 2), start=True, stop=True).then_inc(m["brought"], 1)
                    loop(pe, STEPS // UNROLL, step, UNROLL, drain=2)

                @block.scalar
                def _(act):
                    def step(i, s):
                        k = i * UNROLL + s
                        if not (isinstance(k, int) and k >= STEPS):
                            if s == 0:
                                if not isinstance(i, int):
                                    act.wait_ge(m["turned"], i * UNROLL)
                                    act.sem_inc(m["go"], 0 + 1)
                                nc.scalar.copy(mark[:, :], start_d[:, bass.ds(k, UNROLL)]).then_inc(m["marked"], 1)
                            act.wait_ge(m["turned"], k + 1)
                            nc.scalar.copy(mask(s), tg(s)[:, F:F + P]).then_inc(m["masked"], 1)
                        q = at(i, s, UNROLL, 1)
                        if q is not None:
                            act.wait_ge(m["returned"], q + 1)
                            if at(i, s, UNROLL, 3) is not None:
                                act.wait_ge(m["brought"], at(i, s, UNROLL, 3) + 1)
                            nc.scalar.copy(back(s - 1), tb(s - 1)[:, 0:F]).then_inc(m["lifted"], 1)
                    loop(act, STEPS // UNROLL, step, UNROLL, drain=1)

                @block.vector
                def _(v):
                    v.memset(agg[:, :], 0.0).then_inc(m["added"], 1)
                    v.memset(wrows[:, :], -BIG).then_inc(m["added"], 0 + 1)
                    v.wait_ge(m["added"], 2)
                    def step(i, s, blk):
                        k = i * UNROLL + s
                        if not (isinstance(k, int) and k >= STEPS):
                            if at(i, s, UNROLL, 4) is not None:
                                v.wait_ge(m["brought"], at(i, s, UNROLL, 4) + 1)
                            v.tensor_scalar(oneh(s), iota_f[:, :], last_d[:, bass.ds(k, 1)], None, ALU.is_equal).then_inc(m["made"], 1)
                            v.wait_ge(m["masked"], k + 1)
                            if at(i, s, UNROLL, 2) is not None:
                                v.wait_ge(m["returned"], at(i, s, UNROLL, 2) + 1)
                            if at(i, s, UNROLL, 1) is not None:
                                v.wait_ge(m["scanned"], 2 * at(i, s, UNROLL, 1) + 2)
                            for h in range(2):
                                v.tensor_tensor_scan(run(s, h), mask(s), tg(s)[:, h * P:(h + 1) * P],
                                                     run(s - 1, h)[:, P - 1:P], ALU.add, ALU.max).then_inc(m["scanned"], 1)
                        q = at(i, s, UNROLL, lag)
                        if q is None:
                            return
                        v.wait_ge(m["brought"], q + 1)
                        v.wait_ge(m["added"], q + 2)
                        o = agg[:, bass.ds(blk * W8, F)]
                        v.tensor_tensor(o, o, psum[(s - lag) % 4][:, 0:F], ALU.add).then_inc(m["added"], 1)
                    block_loop(v, block_d, lag, step)


        def in_turn(eng, sem):
            n = [0]

            def do(inst):
                inst.then_inc(sem, 1)
                n[0] += 1
                eng.wait_ge(sem, n[0])
            return do

        row3 = lambda t, w: t.rearrange("t (j e w) -> t j e w", j=CHUNKS, w=w)
        f_gather = agg[:, 0:2048]
        f_row = agg[:, 2048:4096]
        s_row = agg[:, 4096:6144]
        g_row = x_eng[:, 0:4096]
        g_full = ring[:, 0:4096]
        sm_node = small[:, 0:BLOCKS * HEADS]

        def segment_masks():
            any_r = small[:, 0:4]
            st = start_r[:, :].rearrange("t (j e) -> t j e", j=CHUNKS)
            with phase("vec", "turned") as (block, m):
                @block.vector
                def _(v):
                    do = in_turn(v, m["vec"])
                    do(v.tensor_reduce(any_r, st, AX.X, ALU.max))
                    do(v.tensor_scalar(first_keep[:, :], st[:, :, 0], -1.0, 1.0, ALU.mult, ALU.add))
                    do(v.tensor_scalar(first_open[:, :], st[:, :, 0], -BIG, None, ALU.mult))
                    do(v.tensor_scalar(keep_r[:, :], start_r[:, :], -1.0, 1.0, ALU.mult, ALU.add))
                    do(v.tensor_scalar(open_r[:, :], start_r[:, :], -BIG, None, ALU.mult))
                    do(v.memset(keep_r[:, :].rearrange("t (j e) -> t j e", j=CHUNKS)[:, :, 0], 0.0))
                    do(v.memset(open_r[:, :].rearrange("t (j e) -> t j e", j=CHUNKS)[:, :, 0], -BIG))
                    do(v.tensor_copy(small[:, 8:40].rearrange("t (j r) -> t j r", j=CHUNKS),
                                     bc(any_r.unsqueeze(2), [P, CHUNKS, 8])))
                    v.wait_ge(m["turned"], 1)
                    do(v.tensor_scalar(chain_keep[:, :], psum[0][0:8, :], -1.0, 1.0, ALU.mult, ALU.add))
                    do(v.tensor_scalar(chain_open[:, :], psum[0][0:8, :], -BIG, None, ALU.mult))

                @block.tensor
                def _(pe):
                    pe.wait_ge(m["vec"], 8)
                    for j in range(CHUNKS):
                        last = pe.transpose(psum[0][0:8, j * P:(j + 1) * P], small[:, 8 + 8 * j:16 + 8 * j], ident[:, :])
                    last.then_inc(m["turned"], 1)

        def segment_scan(v, pe, data, result, planes, maximum, m):
            mask, chain, first = (open_r, chain_open, first_open) if maximum else (keep_r, chain_keep, first_keep)
            ops = (ALU.add, ALU.max) if maximum else (ALU.mult, ALU.add)
            empty = -BIG if maximum else 0.0
            d4, r4 = row3(data, planes), row3(result, planes)
            d3 = data.rearrange("t (s w) -> t s w", w=planes)
            r3 = result.rearrange("t (s w) -> t s w", w=planes)
            patch = small[:, 128:128 + CHUNKS * planes].rearrange("t (j w) -> t j w", w=planes)

            def vector_part(do):
                def scans():
                    for w in range(planes):
                        do(v.tensor_tensor_scan(r3[:, :, w], mask[:, :], d3[:, :, w], empty, *ops))
                scans()
                v.sem_inc(m["scanned"], 1)
                v.wait_ge(m["turned"], 1)
                do(v.memset(carry[0:planes, 0:1], empty))
                do(v.tensor_tensor_scan(carry[0:planes, 1:], chain[0:planes, :], psum[4][0:planes, :], empty, *ops))
                v.sem_inc(m["scanned"], 1)
                v.wait_ge(m["turned"], 2)
                back = psum[5][:, 0:CHUNKS * planes].rearrange("t (j w) -> t j w", w=planes)
                do(v.tensor_tensor(patch, back, bc(first[:, :].unsqueeze(2), [P, CHUNKS, planes]), ops[0]))
                do(v.tensor_tensor(d4[:, :, 0, :], d4[:, :, 0, :], patch, ops[1]))
                scans()

            def tensor_part():
                pe.wait_ge(m["scanned"], 1)
                for j in range(CHUNKS):
                    last = pe.transpose(psum[4][0:planes, j * P:(j + 1) * P], r4[:, j, P - 1, :], ident[:, :])
                last.then_inc(m["turned"], 1)
                pe.wait_ge(m["scanned"], 2)
                for j in range(CHUNKS):
                    last = pe.transpose(psum[5][:, j * planes:(j + 1) * planes], carry[0:planes, j * P:(j + 1) * P],
                                        ident[0:planes, 0:planes])
                last.then_inc(m["turned"], 1)
            return vector_part, tensor_part

        def node_scores(global_softmax, a_src, a_dst, h):
            hs, prod = heads(h), agg[:, 0:BLOCKS * F]
            with phase("rows_in", "vec", "stored") as (block, m):
                rows_in, vec, stored = (m[x] for x in ("rows_in", "vec", "stored"))

                @block.sync
                def _(sp):
                    for row, a in ((row_a, a_src), (row_b, a_dst)):
                        sp.dma_start(row[:, :].rearrange("p (h c) -> p h c", h=HEADS), bc(a, [P, HEADS, C])).then_inc(rows_in, 16)
                    sp.wait_ge(vec, 4)
                    sp.dma_start(ftable.rearrange("(b p) h -> p b h", p=P), f3).then_inc(stored, 16)
                    sp.wait_ge(stored, 16)

                @block.vector
                def _(v):
                    do = in_turn(v, vec)
                    pad_first = NODES - (BLOCKS - 1) * P
                    src = h
                    do(v.memset(gm_node[:, :], 0.0))
                    if global_softmax:
                        do(v.scalar_tensor_tensor(act_a[:, :], h[:, :], 0.2, h[:, :], ALU.mult, ALU.max))
                        src = act_a
                    else:
                        do(v.memset(small[:, 0:1], 0.0))
                    v.wait_ge(rows_in, 32)
                    for row, o in ((row_a, f3), (row_b, gm4[:, :, 0, :])):
                        do(v.tensor_tensor(prod.rearrange("p (b f) -> p b f", f=F), blocks(src),
                                           bc(row[:, :].unsqueeze(1), [P, BLOCKS, F]), ALU.mult))
                        do(v.tensor_reduce(o, prod.rearrange("p (b h c) -> p b h c", h=HEADS, c=C), AX.X, ALU.add))
                    if global_softmax:
                        do(v.tensor_scalar(small[:, 0:1], iota_p[:, :], float(pad_first), -1e30, ALU.is_ge, ALU.mult))
                        do(v.tensor_scalar(gm4[:, BLOCKS - 1, 0, :], gm4[:, BLOCKS - 1, 0, :], small[:, 0:1], None, ALU.add))

        def gather_scores():
            got = lambda n: wrows[:, n * HEADS:(n + 1) * HEADS]
            G = 400
            with phase("go", "staged", "moved", "cleared", *ROW_SEMS) as (block, m):
                @block.gpsimd
                def _(g):
                    gathers(g, row_t, ftable[:, :], got, m, G, m["moved"])

                @block.vector
                def _(v):
                    v.memset(f_gather[:, G * HEADS:], 0.0).then_inc(m["cleared"], 1)
                    def half(i, h):
                        for n in range(h * 8, h * 8 + 8):
                            v.wait_ge(m[f"row{n}"], i * 16 + 16)
                        v.tensor_copy(f_gather[:, bass.ds((i * 16 + h * 8) * HEADS, 8 * HEADS)],
                                      wrows[:, h * 8 * HEADS:(h + 1) * 8 * HEADS]).then_inc(m["moved"], 8)
                    half(0, 0)
                    half(0, 1)
                    with v.Fori(1, G // 16) as i:
                        half(i, 0)
                        half(i, 1)

        def segment_maxima():
            saved = small[:, 200:216].rearrange("t (j w) -> t j w", w=HEADS)
            with phase("vec", "f_turned", "scanned", "turned", "stored", "read", "cleared") as (block, m):
                fr = f_row.rearrange("t (s w) -> t s w", w=HEADS)
                fr4 = row3(f_row, HEADS)
                parts = {}

                @block.vector
                def _(v):
                    do = in_turn(v, m["vec"])
                    v.wait_ge(m["f_turned"], 1)
                    for h in range(HEADS):
                        do(v.tensor_copy(fr[:, :, h], psum[h][:, :]))
                    do(v.tensor_copy(saved, fr4[:, :, 0, :]))
                    parts["v"], parts["pe"] = segment_scan(v, nc.tensor, f_row, s_row, HEADS, True, m)
                    parts["v"](do)
                    v.sem_inc(m["scanned"], 1)
                    do(v.tensor_copy(fr4[:, :, 0, :], saved))
                    do(v.memset(sm_node, -BIG))
                    v.sem_inc(m["cleared"], 1)

                @block.tensor
                def _(pe):
                    fg = f_gather.rearrange("e (t w) -> e t w", w=HEADS)
                    for h in range(HEADS):
                        for j in range(CHUNKS):
                            last = pe.transpose(psum[h][:, j * P:(j + 1) * P], fg[:, j * P:(j + 1) * P, h], ident[:, :])
                    last.then_inc(m["f_turned"], 1)
                    parts["pe"]()

                @block.sync
                def _(sp):
                    sp.wait_ge(m["scanned"], 3)
                    sp.dma_start(seg_maxima.rearrange("(j t e) h -> t j (e h)", j=CHUNKS, t=P),
                                 s_row.rearrange("t (j e) -> t j e", j=CHUNKS)).then_inc(m["stored"], 16)
                    sp.wait_ge(m["stored"], 16)

                @block.gpsimd
                def _(g):
                    g.wait_ge(m["stored"], 16)
                    g.wait_ge(m["cleared"], 1)
                    for b in range(BLOCKS):
                        g.indirect_dma_start(out=sm_node[:, b * HEADS:(b + 1) * HEADS], out_offset=None, in_=seg_maxima[:, :],
                                             in_offset=bass.IndirectOffsetOnAxis(ap=final_row[:, b:b + 1], axis=0),
                                             bounds_check=SLOTS - 1, oob_is_err=False).then_inc(m["read"], 16)
                    g.wait_ge(m["read"], 16 * BLOCKS)

        def node_shifts(global_softmax):
            sm3 = sm_node.rearrange("p (b h) -> p b h", h=HEADS)
            g3, m3 = gm4[:, :, 0, :], gm4[:, :, 1, :]
            ws3 = w_self[:, :].rearrange("p (b h) -> p b h", h=HEADS)
            top = small[:, 224:228]
            dg = small[0:HEADS, 232:236]
            tmp = wrows[:, 0:BLOCKS * HEADS].rearrange("p (b h) -> p b h", h=HEADS)
            with phase("vec", "top", "turned", "exped", "ready", "sent") as (block, m):
                @block.vector
                def _(v):
                    do = in_turn(v, m["vec"])
                    do(v.tensor_tensor(sm3, sm3, f3, ALU.max))
                    do(v.tensor_tensor(sm3, sm3, g3, ALU.add))
                    if global_softmax:
                        do(v.tensor_reduce(top, sm_node.rearrange("p (b h) -> p h b", h=HEADS), AX.X, ALU.max))
                        v.sem_inc(m["top"], 1)
                        v.wait_ge(m["turned"], 1)
                        do(v.tensor_reduce(small[0:HEADS, 228:229], psum[0][0:HEADS, 0:P], AX.X, ALU.max))
                        do(v.tensor_scalar(dg, ident[0:HEADS, 0:HEADS], small[0:HEADS, 228:229], None, ALU.mult))
                        v.sem_inc(m["top"], 1)
                        v.wait_ge(m["turned"], 2)
                        do(v.tensor_copy(top, psum[1][:, 0:HEADS]))
                        do(v.tensor_tensor(g3, g3, bc(top.unsqueeze(1), [P, BLOCKS, HEADS]), ALU.subtract))
                        do(v.tensor_tensor(tmp, f3, g3, ALU.add))
                    else:
                        do(v.scalar_tensor_tensor(m3, sm3, 0.2, sm3, ALU.mult, ALU.max))
                        do(v.tensor_tensor(sm3, f3, g3, ALU.add))
                        do(v.scalar_tensor_tensor(tmp, sm3, 0.2, sm3, ALU.mult, ALU.max))
                        do(v.tensor_tensor(tmp, tmp, m3, ALU.subtract))
                    v.sem_inc(m["ready"], 1)

                @block.scalar
                def _(act):
                    act.wait_ge(m["ready"], 1)
                    nc.scalar.activation(ws3, tmp, ACT.Exp).then_inc(m["exped"], 1)

                if global_softmax:
                    @block.tensor
                    def _(pe):
                        pe.wait_ge(m["top"], 1)
                        pe.transpose(psum[0][0:HEADS, 0:P], top, ident[:, :]).then_inc(m["turned"], 1)
                        pe.wait_ge(m["top"], 2)
                        pe.matmul(psum[1][:, 0:HEADS], ones[0:HEADS, :], dg, start=True, stop=True).then_inc(m["turned"], 1)

                @block.gpsimd
                def _(g):
                    g.wait_ge(m["ready"], 1)
                    for b in range(BLOCKS):
                        g.indirect_dma_start(out=seg_starts[:, :],
                                             out_offset=bass.IndirectOffsetOnAxis(ap=first_row[:, b:b + 1], axis=0),
                                             in_=gm_node[:, b * 2 * HEADS:(b + 1) * 2 * HEADS], in_offset=None,
                                             bounds_check=SLOTS - 1, oob_is_err=False).then_inc(m["sent"], 16)
                    g.wait_ge(m["sent"], 16 * BLOCKS)

        def edge_weights(global_softmax):
            gf = g_full.rearrange("t (s w) -> t s w", w=2 * HEADS)
            sr = s_row.rearrange("t (s w) -> t s w", w=HEADS)
            fr = f_row.rearrange("t (s w) -> t s w", w=HEADS)
            w3 = w_edge[:, :].rearrange("e (k h) -> e k h", h=HEADS)
            with phase("vec", "loaded", "scanned", "turned", "exped", "picked", "ready") as (block, m):
                parts = {}

                @block.sync
                def _(sp):
                    sp.dma_start(g_row.rearrange("t (j e) -> t j e", j=CHUNKS),
                                 seg_starts.rearrange("(j t e) c -> t j (e c)", j=CHUNKS, t=P)).then_inc(m["loaded"], 16)

                @block.vector
                def _(v):
                    do = in_turn(v, m["vec"])
                    v.wait_ge(m["loaded"], 16)
                    parts["v"], parts["pe"] = segment_scan(v, nc.tensor, g_row, g_full, 2 * HEADS, False, m)
                    parts["v"](do)
                    do(v.tensor_tensor(sr, fr, gf[:, :, 0:HEADS], ALU.add))
                    if not global_softmax:
                        do(v.scalar_tensor_tensor(sr, sr, 0.2, sr, ALU.mult, ALU.max))
                        do(v.tensor_tensor(sr, sr, gf[:, :, HEADS:], ALU.subtract))
                    v.sem_inc(m["ready"], 1)
                    v.wait_ge(m["picked"], 1)
                    for h in range(HEADS):
                        do(v.tensor_copy(w3[:, :, h], psum[h][:, 0:STEPS]))

                @block.scalar
                def _(act):
                    act.wait_ge(m["ready"], 1)
                    nc.scalar.activation(s_row, s_row, ACT.Exp).then_inc(m["exped"], 1)

                @block.tensor
                def _(pe):
                    parts["pe"]()
                    pe.wait_ge(m["exped"], 1)
                    for h in range(HEADS):
                        for j in range(CHUNKS):
                            last = pe.matmul(psum[h][:, 0:STEPS], sr[:, j * P:(j + 1) * P, h], of_step[:, j * STEPS:(j + 1) * STEPS],
                                             start=(j == 0), stop=(j == CHUNKS - 1))
                    last.then_inc(m["picked"], 1)

        def attention(global_softmax, a_src, a_dst):
            node_scores(global_softmax, a_src, a_dst, act_b)
            gather_scores()
            segment_maxima()
            node_shifts(global_softmax)
            edge_weights(global_softmax)
            sum_pass(True, True)

        def attention_out(global_softmax, bias, last):
            ws3 = w_self[:, :].rearrange("p (b h) -> p b h", h=HEADS)
            den = small[:, 0:BLOCKS * HEADS].rearrange("p (b h) -> p b h", h=HEADS)
            total = small[:, 128:132]
            inv = small[:, 132:136]
            ha = heads(act_a)
            shape = [P, BLOCKS, HEADS, C]
            with phase("row_in", "vec", "summed", "ready", "finished") as (block, m):
                @block.sync
                def _(sp):
                    sp.dma_start(row_a[:, :], bc(io[bias].rearrange("(o f) -> o f", o=1), [P, F])).then_inc(m["row_in"], 16)

                @block.vector
                def _(v):
                    do = in_turn(v, m["vec"])
                    do(v.tensor_tensor(den, agg_den, ws3, ALU.add))
                    if global_softmax:
                        do(v.tensor_reduce(total, small[:, 0:BLOCKS * HEADS].rearrange("p (b h) -> p h b", h=HEADS), AX.X, ALU.add))
                        v.sem_inc(m["ready"], 1)
                    else:
                        do(v.reciprocal(small[:, 0:BLOCKS * HEADS], small[:, 0:BLOCKS * HEADS]))
                    do(v.tensor_tensor(ha, heads(act_b), bc(ws3.unsqueeze(3), shape), ALU.mult))
                    do(v.tensor_tensor(ha, ha, agg_h, ALU.add))
                    if global_softmax:
                        v.wait_ge(m["summed"], 1)
                        do(v.reciprocal(inv, psum[0][:, 0:HEADS]))
                        do(v.tensor_tensor(ha, ha, bc(inv.unsqueeze(1).unsqueeze(3), shape), ALU.mult))
                    else:
                        do(v.tensor_tensor(ha, ha, bc(den.unsqueeze(3), shape), ALU.mult))
                    v.wait_ge(m["row_in"], 16)
                    do(v.tensor_tensor(blocks(act_a), blocks(act_a), bc(row_a[:, :].unsqueeze(1), [P, BLOCKS, F]), ALU.add))
                    if not global_softmax:
                        v.sem_inc(m["ready"], 1)
                        v.wait_ge(m["finished"], 1)
                    if last:
                        do(v.tensor_tensor(x_res[:, :], x_res[:, :], act_a[:, :], ALU.add))

                if global_softmax:
                    @block.tensor
                    def _(pe):
                        pe.wait_ge(m["ready"], 1)
                        pe.matmul(psum[0][:, 0:HEADS], ones[:, :], total, start=True, stop=True).then_inc(m["summed"], 1)
                else:
                    @block.scalar
                    def _(act):
                        act.wait_ge(m["ready"], 1)
                        nc.scalar.activation(act_a[:, :], act_a[:, :], ACT.Gelu).then_inc(m["finished"], 1)

        def by_degree(deg, bias=None, plus=None):
            inv, has = small[:, 0:32], small[:, 32:64]
            shape = [P, BLOCKS, F]
            low = agg[:, 0:BLOCKS * F]
            with phase("rows_in", "vec") as (block, m):
                @block.sync
                def _(sp):
                    if bias:
                        sp.dma_start(row_a[:, :], bc(io[bias].rearrange("(o f) -> o f", o=1), [P, F])).then_inc(m["rows_in"], 16)
                        sp.dma_start(slope[:, :], bc(io["L3_gnn_a"].rearrange("(o f) -> o f", o=1), [P, 1])).then_inc(m["rows_in"], 16)
                        sp.wait_ge(m["rows_in"], 32)

                @block.vector
                def _(v):
                    do = in_turn(v, m["vec"])
                    do(v.tensor_scalar(has, deg[:, :], 0.0, None, ALU.is_gt))
                    do(v.tensor_scalar(inv, deg[:, :], 1.0, None, ALU.max))
                    do(v.reciprocal(inv, inv))
                    do(v.tensor_tensor(inv, inv, has, ALU.mult))
                    do(v.tensor_tensor(blocks(act_b), agg_f, bc(inv[:, 0:BLOCKS].unsqueeze(2), shape), ALU.mult))
                    if bias:
                        v.wait_ge(m["rows_in"], 32)
                        do(v.tensor_tensor(blocks(act_b), blocks(act_b), bc(row_a[:, :].unsqueeze(1), shape), ALU.add))
                        if plus is not None:
                            do(v.tensor_tensor(act_b[:, :], act_b[:, :], plus[:, :], ALU.add))
                        do(v.tensor_scalar(low, act_b[:, :], 0.0, slope[:, 0:1], ALU.min, ALU.mult))
                        do(v.scalar_tensor_tensor(act_b[:, :], act_b[:, :], 0.0, low, ALU.max, ALU.add))
                        if plus is not None:
                            do(v.tensor_tensor(x_res[:, :], x_res[:, :], act_b[:, :], ALU.add))

        def hconv(weights_name, source, bias, plus=None):
            load_weights(weights_name, False)
            linear([source], act_b, to_table=True)
            sum_pass(True, False)
            by_degree(deg_d)
            store_table(act_b)
            sum_pass(False, False)
            by_degree(deg_s, bias, plus)

        def store_out():
            with phase("stored") as (block, m):
                @block.sync
                def _(sp):
                    full = (BLOCKS - 1) * P
                    sp.dma_start(out[0:full, :].rearrange("(b p) f -> p b f", p=P), blocks(x_res)[:, 0:BLOCKS - 1, :]).then_inc(m["stored"], 16)
                    sp.dma_start(out[full:NODES, :], x_res[0:NODES - full, (BLOCKS - 1) * F:]).then_inc(m["stored"], 16)
                    sp.wait_ge(m["stored"], 32)

        setup()
        split_keys()
        count()
        places()
        scatter_pairs()
        walk_tables(False)
        walk_tables(True)
        segment_masks()

        layernorm(x_res, act_a)
        load_weights("L0_gnn_Wp1", True)
        linear([act_a], act_b, bias="L0_gnn_bp1", relu=True, to_table=True)
        max_pass()
        load_weights("L0_gnn_Wm1", True)
        linear([act_a, agg], act_b, bias="L0_gnn_bm1", relu=True, to_table=True)
        max_pass()
        load_weights("L0_gnn_Wm2", True)
        linear([act_b, agg], act_a, bias="L0_gnn_bm2", plus=act_b)
        layernorm(act_a, act_a, affine=("L0_gnn_ln2_g", "L0_gnn_ln2_b"))
        store_table(act_a)
        max_pass()
        load_weights("L0_gnn_Wm3", True)
        linear([act_a, agg], act_b, bias="L0_gnn_bm3", plus=act_a)
        layernorm(act_b, act_b, affine=("L0_gnn_ln3_g", "L0_gnn_ln3_b"), add_to=x_res)

        layernorm(x_res, act_a)
        load_weights("L1_gnn_W", False)
        linear([act_a], act_b, to_table=True)
        att = io["L1_gnn_att"]
        attention(True, att[0:1, :, 0:C], att[0:1, :, C:2 * C])
        attention_out(True, "L1_gnn_b", True)

        layernorm(x_res, act_a)
        for n in ("0", "1"):
            load_weights("L2_gnn_W" + n, False)
            linear([act_a], act_b, to_table=True)
            attention(False, *(io["L2_gnn_a_" + k + n].rearrange("(o h) c -> o h c", o=1) for k in ("src", "dst")))
            attention_out(False, "L2_gnn_b" + n, n == "1")

        layernorm(x_res, act_a)
        hconv("L3_gnn_W1", act_a, "L3_gnn_b1")
        hconv("L3_gnn_W2", act_b, "L3_gnn_b2", plus=act_a)
        store_out()


INPUTS = ["x", "src", "dst", "L0_gnn_Wp1", "L0_gnn_bp1", "L0_gnn_Wm1", "L0_gnn_bm1", "L0_gnn_Wm2", "L0_gnn_bm2",
          "L0_gnn_Wm3", "L0_gnn_bm3", "L0_gnn_ln2_g", "L0_gnn_ln2_b", "L0_gnn_ln3_g", "L0_gnn_ln3_b",
          "L1_gnn_W", "L1_gnn_att", "L1_gnn_b", "L2_gnn_W0", "L2_gnn_a_src0", "L2_gnn_a_dst0", "L2_gnn_b0",
          "L2_gnn_W1", "L2_gnn_a_src1", "L2_gnn_a_dst1", "L2_gnn_b1", "L3_gnn_W1", "L3_gnn_b1", "L3_gnn_W2",
          "L3_gnn_b2", "L3_gnn_a"]


def kernel(**inputs):
    import numpy as np
    import concourse.bacc as bacc
    from concourse.bass_utils import run_bass_kernel_spmd

    nc = bacc.Bacc("TRN2", target_bir_lowering=False, num_devices=1)
    arrays, io = {}, {}
    for name in INPUTS:
        a = np.ascontiguousarray(inputs[name])
        arrays["in_" + name] = a
        io[name] = nc.dram_tensor("in_" + name, a.shape, mybir.dt.from_np(a.dtype), kind="ExternalInput").ap()
    out = nc.dram_tensor("out", (NODES, F), F32, kind="ExternalOutput").ap()
    build(nc, io, out)
    result = run_bass_kernel_spmd(nc, [arrays], core_ids=[0])
    return result.results[0]["out"]
```

```python
from contextlib import ExitStack, contextmanager

import concourse.bass as bass
import concourse.mybir as mybir

F32 = mybir.dt.float32
BF16 = mybir.dt.bfloat16
I32 = mybir.dt.int32
ALU = mybir.AluOpType
ACT = mybir.ActivationFunctionType
AX = mybir.AxisListType
DVE = mybir.EngineType.DVE

P = 128
NODES, F = 3125, 256
EDGES = 50000
HEADS = 4
C = F // HEADS
BLOCKS = -(-NODES // P)
ROWS = BLOCKS * P
PAD = ROWS - 1
TILES = 392
CHUNKS = 4
SLOTS = CHUNKS * P * P
STEPS = TILES + BLOCKS - 1
UNROLL = 16
LAG = 4
BIG = float(2.0 ** 126)
FAR = 8192.0
OUTSIDE = 100000.0
W8 = F + HEADS


def build(nc, io, out):
    ctx = ExitStack()
    phases = [0]

    def sb(name, shape, dt=F32):
        return ctx.enter_context(nc.sbuf_tensor(name, shape, dt))

    @contextmanager
    def phase(*names):
        phases[0] += 1
        sems = {n: nc.alloc_semaphore(f"{n}_{phases[0]}") for n in names}
        with nc.Block() as block:
            yield block, sems
        nc.clear_and_free_semaphores(list(sems.values()))
        nc.all_engine_barrier()

    def loop(eng, total, step, unroll, drain=0):
        rounds = total // unroll
        for s in range(unroll):
            step(0, s)
        if rounds > 1:
            with eng.Fori(1, rounds) as i:
                for s in range(unroll):
                    step(i, s)
        for s in range(total - rounds * unroll + drain):
            step(rounds, s)

    def live(k, total):
        return k is not None and not (isinstance(k, int) and k >= total)

    def at(i, s, unroll, back=0):
        k = i * unroll + s - back
        return None if isinstance(k, int) and k < 0 else k

    with ctx:
        dst_list = nc.dram_tensor("dst_list", (1 + EDGES + 122 * P,), I32).ap()
        src_list = nc.dram_tensor("src_list", (1 + EDGES + 122 * P,), I32).ap()
        pair_list = nc.dram_tensor("pair_list", (1 + TILES * P + 121 * P, 2), I32).ap()
        table = nc.dram_tensor("table", (ROWS, F), F32).ap()
        seg_starts = nc.dram_tensor("seg_starts", (SLOTS, 2 * HEADS), F32).ap()
        low_turned = nc.dram_tensor("low_turned", (P, TILES * P), BF16).ap()
        high_kept = nc.dram_tensor("high_kept", (P, TILES * 32), BF16).ap()
        seg_maxima = nc.dram_tensor("seg_maxima", (SLOTS, HEADS), F32).ap()

        psum = [ctx.enter_context(nc.psum_tensor(f"bank{n}", [P, 512], F32)) for n in range(8)]

        x_res = sb("x_res", [P, BLOCKS * F])
        act_a = sb("act_a", [P, BLOCKS * F])
        act_b = sb("act_b", [P, BLOCKS * F])
        agg = sb("agg", [P, BLOCKS * W8])
        ring = sb("ring", [P, UNROLL * F])
        wrows = sb("wrows", [P, 4 * W8])
        onehot = sb("onehot", [P, 4 * P])
        weights = sb("weights", [P, 4 * F])
        row_a = sb("row_a", [P, F])
        row_b = sb("row_b", [P, F])
        ident = sb("ident", [P, P])
        ident_b = sb("ident_b", [P, P], BF16)
        iota_f = sb("iota_f", [P, P])
        iota_b = sb("iota_b", [P, P], BF16)
        iota_p = sb("iota_p", [P, 1])
        ones = sb("ones", [P, P])
        below = sb("below", [P, P])
        tile_no = sb("tile_no", [P, CHUNKS * P])
        step_no = sb("step_no", [P, STEPS])
        of_step = sb("of_step", [P, CHUNKS * STEPS])
        node_d = sb("node_d", [P, STEPS])
        last_d = sb("last_d", [P, STEPS])
        start_d = sb("start_d", [P, STEPS])
        row_d = sb("row_d", [P, STEPS], I32)
        block_d = sb("block_d", [P, STEPS + UNROLL], I32)
        by_src = sb("by_src", [P, 3 * STEPS + UNROLL])
        node_s = by_src[:, 0:STEPS]
        row_s = by_src[:, STEPS:2 * STEPS].bitcast(I32)
        block_s = by_src[:, 2 * STEPS:].bitcast(I32)
        pair = by_src[:, 0:2 * TILES].bitcast(I32)
        place = by_src[:, 2 * TILES:3 * TILES].bitcast(I32)
        start_r = sb("start_r", [P, CHUNKS * P])
        deg_d = sb("deg_d", [P, 32])
        deg_s = sb("deg_s", [P, 32])
        first_s = sb("first_s", [P, 32])
        first_row = sb("first_row", [P, BLOCKS], I32)
        final_row = sb("final_row", [P, BLOCKS], I32)
        f_node = sb("f_node", [P, BLOCKS * HEADS])
        gm_node = sb("gm_node", [P, BLOCKS * 2 * HEADS])
        w_self = sb("w_self", [P, BLOCKS * HEADS])
        w_edge = sb("w_edge", [P, STEPS * HEADS])
        slope = sb("slope", [P, 1])
        keep_r = sb("keep_r", [P, CHUNKS * P])
        open_r = sb("open_r", [P, CHUNKS * P])
        chain_keep = sb("chain_keep", [8, CHUNKS * P])
        chain_open = sb("chain_open", [8, CHUNKS * P])
        carry = sb("carry", [8, 1 + CHUNKS * P])
        first_keep = sb("first_keep", [P, CHUNKS])
        first_open = sb("first_open", [P, CHUNKS])
        small = sb("small", [P, 256])
        stage_i = sb("stage_i", [P, 2 * UNROLL], I32)
        node_st = sb("node_st", [P, UNROLL])
        mark = sb("mark", [P, UNROLL], BF16)
        x_eng = sb("work", [P, 12 * 512])

        def bc(ap, shape):
            return ap.to_broadcast(shape)

        def blocks(t):
            return t[:, 0:BLOCKS * F].rearrange("p (b f) -> p b f", f=F)

        def heads(t):
            return t[:, 0:BLOCKS * F].rearrange("p (b h c) -> p b h c", h=HEADS, c=C)

        agg3 = agg[:, :].rearrange("p (b w) -> p b w", w=W8)
        agg_f = agg3[:, :, 0:F]
        agg_h = agg_f.rearrange("p b (h c) -> p b h c", h=HEADS)
        agg_den = agg3[:, :, F:W8]
        f3 = f_node[:, :].rearrange("p (b h) -> p b h", h=HEADS)
        gm4 = gm_node[:, :].rearrange("p (b g h) -> p b g h", g=2, h=HEADS)
        table_v = table.rearrange("(b p) f -> p b f", p=P)

        def setup():
            with phase("made", "cast", "x_in", "pads", "lists_in") as (block, m):
                made, cast, x_in, pads, lists_in = (m[n] for n in ("made", "cast", "x_in", "pads", "lists_in"))
                pad_i = x_eng[:, 0:256].bitcast(I32)
                first_i = x_eng[:, 256:257].bitcast(I32)

                @block.gpsimd
                def _(g):
                    g.iota(iota_f[:, :], pattern=[[1, P]], base=0, channel_multiplier=0,
                           allow_small_or_imprecise_dtypes=True).then_inc(made, 1)
                    g.iota(iota_p[:, :], pattern=[[0, 1]], base=0, channel_multiplier=1,
                           allow_small_or_imprecise_dtypes=True).then_inc(made, 1)
                    g.iota(tile_no[:, :], pattern=[[P, CHUNKS], [0, P]], base=0, channel_multiplier=1,
                           allow_small_or_imprecise_dtypes=True).then_inc(made, 1)
                    g.iota(step_no[:, :], pattern=[[1, STEPS]], base=0, channel_multiplier=0,
                           allow_small_or_imprecise_dtypes=True).then_inc(made, 1)
                    g.iota(pad_i, pattern=[[0, 256]], base=PAD, channel_multiplier=0).then_inc(made, 1)
                    g.iota(first_i, pattern=[[0, 1]], base=-1, channel_multiplier=0).then_inc(made, 1)

                @block.vector
                def _(v):
                    v.memset(ones[:, :], 1.0).then_inc(cast, 1)
                    v.memset(x_res[:, (BLOCKS - 1) * F:], 0.0).then_inc(pads, 1)
                    v.wait_ge(made, 6)
                    v.tensor_copy(iota_b[:, :], iota_f[:, :]).then_inc(cast, 1)
                    v.tensor_scalar(ident[:, :], iota_f[:, :], iota_p[:, 0:1], None, ALU.is_equal).then_inc(cast, 1)
                    v.tensor_scalar(ident_b[:, :], iota_f[:, :], iota_p[:, 0:1], None, ALU.is_equal).then_inc(cast, 1)
                    v.tensor_scalar(below[:, :], iota_f[:, :], iota_p[:, 0:1], None, ALU.is_gt).then_inc(cast, 1)
                    v.memset(x_eng[:, 512:], 0.0).then_inc(cast, 1)

                @block.sync
                def _(sp):
                    full = (BLOCKS - 1) * P
                    sp.dma_start(blocks(x_res)[:, 0:BLOCKS - 1, :],
                                 io["x"][0:full, :].rearrange("(b p) f -> p b f", p=P)).then_inc(x_in, 16)
                    for name, lst in (("dst", dst_list), ("src", src_list)):
                        sp.dma_start(lst[1:1 + EDGES].rearrange("(a b) -> a b", a=16),
                                     io[name].rearrange("(a b) -> a b", a=16)).then_inc(lists_in, 16)
                    sp.wait_ge(pads, 1)
                    sp.dma_start(x_res[0:NODES - full, (BLOCKS - 1) * F:], io["x"][full:NODES, :]).then_inc(x_in, 16)
                    sp.wait_ge(made, 6)
                    for lst in (dst_list, src_list):
                        sp.dma_start(lst[1 + EDGES:].rearrange("(a b) -> a b", b=P), pad_i[0:122, 0:P]).then_inc(lists_in, 16)
                        sp.dma_start(lst[0:1].rearrange("(a b) -> a b", a=1), first_i[0:1, :]).then_inc(lists_in, 16)
                    pl = pair_list[1 + TILES * P:, :].rearrange("(a b) c -> a (b c)", b=P)
                    sp.dma_start(pl, pad_i[0:121, :]).then_inc(lists_in, 16)
                    sp.dma_start(pair_list[0:1, 0:1], first_i[0:1, :]).then_inc(lists_in, 16)
                    sp.dma_start(pair_list[0:1, 1:2], first_i[0:1, :]).then_inc(lists_in, 16)
                    zero = x_eng[:, 512:512 + 4096]
                    sp.wait_ge(cast, 6)
                    sp.dma_start(seg_starts.rearrange("(p a) c -> p (a c)", p=P), zero).then_inc(lists_in, 16)
                    sp.wait_ge(x_in, 32)
                    sp.wait_ge(lists_in, 16 * 10)

        def row_load(sp, tile, lst, off, sem):
            n = lst.shape[1] if len(lst.shape) > 1 else 1
            if n == 1:
                src = lst[off:off + SLOTS].rearrange("(j t e) -> t j e", j=CHUNKS, t=P)
                sp.dma_start(tile.rearrange("t (j e) -> t j e", j=CHUNKS), src).then_inc(sem, 16)
            else:
                src = lst[off:off + SLOTS, :].rearrange("(j t e) c -> t j (e c)", j=CHUNKS, t=P)
                sp.dma_start(tile.rearrange("t (j e) -> t j e", j=CHUNKS), src).then_inc(sem, 16)

        def walk_tables(by_dst):
            node_k, row_k, block_k = (node_d, row_d, block_d) if by_dst else (node_s, row_s, block_s)
            w = 512 if by_dst else 1024
            raw = [x_eng[:, n * w:(n + 1) * w].bitcast(I32) for n in range(4)]
            if by_dst:
                key_i, prev_i, next_i, pay_i = raw
            else:
                key_i, prev_i, next_i = (r.rearrange("t (s c) -> t s c", c=2)[:, :, 0] for r in raw[0:3])
                pay_i = raw[0].rearrange("t (s c) -> t s c", c=2)[:, :, 1]
            vals = [x_eng[:, 3072 + n * 512:3584 + n * 512] for n in range(5)]
            key_f, prev_f, next_f, pay_f, last_f = vals
            lo_i = small[:, 0:4].bitcast(I32)
            hi_i = small[:, 4:8].bitcast(I32)
            lo = small[:, 8:12]
            hi = small[:, 12:16]
            tno = tile_no[:, :].rearrange("t (j e) -> t j e", e=P)[:, :, 0]
            with phase("loaded", "cast", "ready", "summed", "done") as (block, m):
                loaded, cast, ready, summed, done = (m[n] for n in ("loaded", "cast", "ready", "summed", "done"))

                @block.sync
                def _(sp):
                    if by_dst:
                        row_load(sp, key_i, dst_list, 1, loaded)
                        row_load(sp, prev_i, dst_list, 0, loaded)
                        row_load(sp, next_i, dst_list, 2, loaded)
                        row_load(sp, pay_i, src_list, 1, loaded)
                    else:
                        row_load(sp, raw[0], pair_list, 1, loaded)
                        row_load(sp, raw[1], pair_list, 0, loaded)
                        row_load(sp, raw[2], pair_list, 2, loaded)

                @block.vector
                def _(v):
                    v.memset(block_k[:, 0:LAG], 0).then_inc(done, 1)
                    v.memset(block_k[:, LAG + STEPS:], 0).then_inc(done, 1)
                    v.wait_ge(loaded, 64 if by_dst else 48)
                    for o, i in ((key_f, key_i), (prev_f, prev_i), (next_f, next_i), (pay_f, pay_i)):
                        v.tensor_copy(o, i).then_inc(cast, 1)
                    kk = raw[0].rearrange("t (j e) -> t j e", j=CHUNKS)
                    pp = raw[1].rearrange("t (j e) -> t j e", j=CHUNKS)
                    last_at = (P - 1) * (1 if by_dst else 2)
                    v.tensor_single_scalar(hi_i, kk[:, :, last_at], 7, op=ALU.arith_shift_right).then_inc(cast, 1)
                    v.tensor_single_scalar(lo_i, pp[:, :, 0], 7, op=ALU.arith_shift_right).then_inc(cast, 1)
                    v.wait_ge(cast, 6)
                    v.tensor_tensor(hi, hi_i, tno, ALU.add).then_inc(cast, 1)
                    v.tensor_tensor(lo, lo_i, tno, ALU.add).then_inc(cast, 1)
                    v.wait_ge(cast, 8)
                    for j in range(CHUNKS):
                        v.tensor_scalar(of_step[:, j * STEPS:(j + 1) * STEPS], step_no[:, :], lo[:, j:j + 1], None,
                                        ALU.is_ge).then_inc(cast, 1)
                    v.wait_ge(cast, 12)
                    for j in range(CHUNKS):
                        o = of_step[:, j * STEPS:(j + 1) * STEPS]
                        v.scalar_tensor_tensor(o, step_no[:, :], hi[:, j:j + 1], o, ALU.is_le, ALU.mult).then_inc(ready, 1)
                    if by_dst:
                        v.tensor_tensor(last_f, key_f, next_f, ALU.not_equal).then_inc(cast, 1)
                        v.tensor_tensor(start_r[:, :], key_f, prev_f, ALU.not_equal).then_inc(ready, 1)
                        v.wait_ge(cast, 13)
                        v.scalar_tensor_tensor(last_f, key_f, FAR, last_f, ALU.add, ALU.mult).then_inc(cast, 1)
                        v.wait_ge(cast, 14)
                        v.tensor_scalar(last_f, last_f, -FAR, None, ALU.add).then_inc(ready, 1)
                    v.wait_ge(summed, 1)
                    blk = x_eng[:, 0:STEPS]
                    v.tensor_tensor(blk, step_no[:, :], psum[0][:, 0:STEPS], ALU.subtract).then_inc(done, 1)
                    v.wait_ge(done, 3)
                    v.tensor_copy(block_k[:, LAG:LAG + STEPS], blk).then_inc(done, 1)
                    v.tensor_copy(row_k[:, :], psum[2][:, 0:STEPS]).then_inc(done, 1)
                    v.scalar_tensor_tensor(node_k[:, :], blk, -float(P), psum[1][:, 0:STEPS], ALU.mult, ALU.add).then_inc(done, 1)
                    if by_dst:
                        v.scalar_tensor_tensor(last_d[:, :], blk, -float(P), psum[3][:, 0:STEPS], ALU.mult, ALU.add).then_inc(done, 1)
                        v.tensor_scalar(start_d[:, :], psum[4][:, 0:STEPS], -BIG, None, ALU.mult).then_inc(done, 1)

                @block.tensor
                def _(pe):
                    pe.wait_ge(ready, 6 if by_dst else 4)
                    rows = [tile_no[:, :], key_f, pay_f] + ([last_f, start_r[:, :]] if by_dst else [])
                    for n, r in enumerate(rows):
                        for j in range(CHUNKS):
                            last = pe.matmul(psum[n][:, 0:STEPS], r[:, j * P:(j + 1) * P], of_step[:, j * STEPS:(j + 1) * STEPS],
                                             start=(j == 0), stop=(j == CHUNKS - 1))
                    last.then_inc(summed, 1)

        G8 = 8
        GROUPS = TILES // G8
        KEYS = 4
        keys = x_eng[:, 0:CHUNKS * P * KEYS // 2].bitcast(BF16)
        key3 = keys.rearrange("p (t k) -> p t k", k=KEYS)

        def split_keys():
            raw = [act_a[:, n * 512:512 + n * 512].bitcast(I32) for n in range(2)]
            part = [act_a[:, 1024 + n * 512:1536 + n * 512].bitcast(I32) for n in range(4)]
            val = [act_a[:, 3072 + n * 512:3584 + n * 512] for n in range(6)]
            pair3 = pair.rearrange("p (t c) -> p t c", c=2)
            with phase("loaded", "cast", "turned", "done") as (block, m):
                loaded, cast, turned, done = (m[n] for n in ("loaded", "cast", "turned", "done"))

                @block.sync
                def _(sp):
                    row_load(sp, raw[0], dst_list, 1, loaded)
                    row_load(sp, raw[1], src_list, 1, loaded)

                @block.vector
                def _(v):
                    v.wait_ge(loaded, 32)
                    for n in range(2):
                        v.tensor_single_scalar(part[2 * n], raw[n], 127, op=ALU.bitwise_and).then_inc(cast, 1)
                        v.tensor_single_scalar(part[2 * n + 1], raw[n], 7, op=ALU.arith_shift_right).then_inc(cast, 1)
                    v.wait_ge(cast, 4)
                    for n in range(4):
                        v.tensor_copy(val[n], part[n]).then_inc(cast, 1)
                    for n in range(2):
                        v.tensor_copy(val[4 + n], raw[n]).then_inc(cast, 1)
                    v.wait_ge(turned, 1)
                    for n in range(4):
                        v.tensor_copy(key3[:, :, n], psum[n][:, :]).then_inc(done, 1)
                    for n in range(2):
                        v.tensor_copy(pair3[:, :, n], psum[5 - n][:, 0:TILES]).then_inc(done, 1)

                @block.tensor
                def _(pe):
                    pe.wait_ge(cast, 10)
                    for n in range(6):
                        for j in range(CHUNKS):
                            last = pe.transpose(psum[n][:, j * P:(j + 1) * P], val[n][:, j * P:(j + 1) * P], ident[:, :])
                    last.then_inc(turned, 1)

        def one_hots(v, low, high, key, made):
            v.tensor_tensor(low.rearrange("p (t e) -> p t e", e=P), bc(iota_b[:, :].unsqueeze(1), [P, G8, P]),
                            bc(key[:, :, 0:1], [P, G8, P]), ALU.is_equal).then_inc(made, 1)
            v.tensor_tensor(high.rearrange("p (t b) -> p t b", b=32), bc(iota_b[:, 0:32].unsqueeze(1), [P, G8, 32]),
                            bc(key[:, :, 1:2], [P, G8, 32]), ALU.is_equal).then_inc(made, 1)

        def count():
            low = lambda s, n: act_a[:, (s % 2 * 2 + n) * 512:(s % 2 * 2 + n + 1) * 512].bitcast(BF16)
            high = lambda s, n: act_a[:, 2048 + (s % 2 * 2 + n) * 128:2048 + (s % 2 * 2 + n + 1) * 128].bitcast(BF16)
            with phase("made", "counted", "copied", "totals", "done") as (block, m):
                made, counted, copied, totals, done = (m[n] for n in ("made", "counted", "copied", "totals", "done"))

                @block.vector
                def _(v):
                    def step(i, s):
                        if at(i, s, 2, 2) is not None:
                            v.wait_ge(counted, at(i, s, 2, 2) + 1)
                            v.wait_ge(made, 4 * at(i, s, 2, 2) + 4)
                        for n in range(2):
                            one_hots(v, low(s, n), high(s, n), key3[:, bass.ds(at(i, s, 2) * G8, G8), 2 * n:2 * n + 2], made)
                    loop(v, GROUPS, step, 2)
                    v.wait_ge(counted, GROUPS)
                    v.tensor_copy(deg_d[:, :], psum[0][:, 0:32]).then_inc(copied, 1)
                    v.tensor_copy(deg_s[:, :], psum[1][:, 0:32]).then_inc(copied, 1)
                    v.wait_ge(totals, 1)
                    tot = small[:, 0:64]
                    inc = small[:, 64:128]
                    pos_ = small[:, 128:160]
                    fst = small[:, 160:192]
                    fin = small[:, 192:224]
                    v.tensor_copy(tot, psum[2][:, 0:64]).then_inc(done, 1)
                    v.wait_ge(done, 1)
                    for n in range(2):
                        v.tensor_tensor_scan(inc[:, 32 * n:32 * n + 32], ones[:, 0:32], tot[:, 32 * n:32 * n + 32], 0.0,
                                             ALU.mult, ALU.add).then_inc(done, 1)
                    v.wait_ge(done, 3)
                    v.tensor_tensor(inc, inc, tot, ALU.subtract).then_inc(done, 1)
                    v.wait_ge(done, 4)
                    v.tensor_tensor(fst, inc[:, 0:32], psum[3][:, 0:32], ALU.add).then_inc(done, 1)
                    v.tensor_tensor(first_s[:, :], inc[:, 32:64], psum[3][:, 32:64], ALU.add).then_inc(done, 1)
                    v.tensor_scalar(pos_, deg_d[:, :], 0.0, None, ALU.is_gt).then_inc(done, 1)
                    v.wait_ge(done, 7)
                    v.scalar_tensor_tensor(fin, fst, -1.0 - OUTSIDE, deg_d[:, :], ALU.add, ALU.add).then_inc(done, 1)
                    v.wait_ge(done, 8)
                    v.tensor_tensor(fin, fin, pos_, ALU.mult).then_inc(done, 1)
                    v.scalar_tensor_tensor(fst, fst, -OUTSIDE, pos_, ALU.add, ALU.mult).then_inc(done, 1)
                    v.wait_ge(done, 10)
                    v.tensor_scalar(first_row[:, :], fst[:, 0:BLOCKS], OUTSIDE, None, ALU.add).then_inc(done, 1)
                    v.tensor_scalar(final_row[:, :], fin[:, 0:BLOCKS], OUTSIDE, None, ALU.add).then_inc(done, 1)

                @block.tensor
                def _(pe):
                    def step(i, s):
                        first = isinstance(i, int) and i == 0 and s == 0
                        pe.wait_ge(made, at(i, s, 2) * 4 + 4)
                        for u in range(G8):
                            for n in range(2):
                                last = pe.matmul(psum[n][:, 0:32], low(s, n)[:, u * P:(u + 1) * P], high(s, n)[:, u * 32:(u + 1) * 32],
                                                 start=(first and u == 0), stop=False, skip_group_check=True)
                        last.then_inc(counted, 1)
                    loop(pe, GROUPS, step, 2)
                    pe.wait_ge(copied, 2)
                    for w, bank in ((ones, psum[2]), (below, psum[3])):
                        pe.matmul(bank[:, 0:32], w[:, :], deg_d[:, :], start=True, stop=True)
                        last = pe.matmul(bank[:, 32:64], w[:, :], deg_s[:, :], start=True, stop=True)
                    last.then_inc(totals, 1)

        def sort_by_src():
            def cut(tile, base, size, dt=F32, slots=2):
                return lambda s: tile[:, base + s % slots * size:base + (s % slots + 1) * size].bitcast(dt)
            low, high = cut(act_a, 0, 512, BF16, 4), cut(act_a, 2048, 128, BF16, 4)
            same, seen, prod, pos_f = cut(act_a, 2560, 512, BF16), cut(act_a, 3584, 288), cut(act_a, 4352, 256), cut(act_a, 5248, 8)
            lowt_b, lowt = cut(act_b, 0, 512, BF16, 4), cut(act_b, 2048, 1024)
            turn = psum[0][:, :].bitcast(BF16)
            hist, looked_up = psum[1], (psum[2], psum[5])
            pairs = [psum[3], psum[4]]
            names = ("made", "turned", "lifted", "counted", "based", "snapped", "paired", "masked", "looked", "summed",
                     "placed", "kept0", "kept1", "kept2", "kept3")
            with phase(*names) as (block, m):
                kept = [m[f"kept{n}"] for n in range(4)]

                @block.vector
                def _(v):
                    v.tensor_copy(seen(1)[:, 256:288], first_s[:, :]).then_inc(m["snapped"], 1)
                    def bases(q, r):
                        sn = seen(r).rearrange("p (t b) -> p t b", b=32)
                        v.wait_ge(m["snapped"], q + 1)
                        v.tensor_copy(sn[:, 0, :], seen(r + 1)[:, 256:288]).then_inc(m["based"], 1)
                        v.wait_ge(m["based"], q + 1)
                        v.wait_ge(m["counted"], q + 1)
                        v.tensor_tensor(sn[:, 1:, :], hist[:, 32:288].rearrange("p (t b) -> p t b", b=32),
                                        bc(sn[:, 0:1, :], [P, G8, 32]), ALU.add).then_inc(m["snapped"], 1)
                        v.wait_ge(m["paired"], q + 1)
                        for n in range(2):
                            v.tensor_tensor(same(r)[:, n * 512:(n + 1) * 512].rearrange("p (t e) -> p t e", e=P),
                                            pairs[n][:, :].rearrange("p (t e) -> p t e", e=P),
                                            bc(below[:, :].unsqueeze(1), [P, 4, P]), ALU.mult).then_inc(m["masked"], 1)

                    def places(q, r):
                        v.wait_ge(m["looked"], q + 1)
                        v.tensor_tensor(prod(r), looked_up[r % 2][:, 0:256], high(r), ALU.mult).then_inc(m["summed"], 1)
                        v.wait_ge(m["summed"], 2 * q + 1)
                        v.tensor_reduce(pos_f(r), prod(r).rearrange("p (t b) -> p t b", b=32), AX.X, ALU.add).then_inc(m["summed"], 1)
                        v.wait_ge(m["summed"], 2 * q + 2)
                        v.tensor_scalar(place[:, bass.ds(q * G8, G8)], pos_f(r), 1.0, None, ALU.add).then_inc(m["placed"], 1)

                    def step(i, s):
                        q = at(i, s, 4, 2)
                        if live(q, GROUPS):
                            bases(q, s + 2)
                        g = at(i, s, 4)
                        if live(g, GROUPS):
                            if at(i, s, 4, 4) is not None:
                                v.wait_ge(m["looked"], at(i, s, 4, 4) + 1)
                                v.wait_ge(kept[s], i * 32)
                                v.wait_ge(m["summed"], 2 * at(i, s, 4, 4) + 2)
                            one_hots(v, low(s), high(s), key3[:, bass.ds(g * G8, G8), 2:4], m["made"])
                        if at(i, s, 4, 3) is not None:
                            places(at(i, s, 4, 3), s + 1)
                    loop(v, GROUPS, step, 4, drain=3)

                @block.tensor
                def _(pe):
                    def first_half(i, s):
                        g = at(i, s, 4)
                        pe.wait_ge(m["made"], 2 * g + 2)
                        if at(i, s, 4, 1) is not None:
                            pe.wait_ge(m["lifted"], 2 * at(i, s, 4, 1) + 2)
                        for u in range(G8):
                            last = pe.transpose(turn[:, u * P:(u + 1) * P], low(s)[:, u * P:(u + 1) * P], ident_b[:, :])
                        last.then_inc(m["turned"], 1)
                        if at(i, s, 4, 1) is not None:
                            pe.wait_ge(m["snapped"], at(i, s, 4, 1) + 2)
                        for u in range(G8):
                            last = pe.matmul(hist[:, (u + 1) * 32:288].rearrange("p (t b) -> p t b", b=32), low(s)[:, u * P:(u + 1) * P],
                                             bc(high(s)[:, u * 32:(u + 1) * 32].unsqueeze(1), [P, G8 - u, 32]),
                                             start=(u == 0), stop=(u == G8 - 1), skip_group_check=True)
                        last.then_inc(m["counted"], 1)

                    def step(i, s):
                        g, q = at(i, s, 4), at(i, s, 4, 1)
                        r = s + 3
                        if q is not None:
                            pe.wait_ge(m["lifted"], 2 * q + 2)
                            if at(i, s, 4, 2) is not None:
                                pe.wait_ge(m["masked"], 2 * at(i, s, 4, 2) + 2)
                            for u in range(G8):
                                lt = lowt_b(r)[:, u * P:(u + 1) * P]
                                last = pe.matmul(pairs[u // 4][:, u % 4 * P:(u % 4 + 1) * P], lt, lt, start=True, stop=True)
                            last.then_inc(m["paired"], 1)
                        if live(g, GROUPS):
                            first_half(i, s)
                        if q is not None:
                            pe.wait_ge(m["snapped"], q + 2)
                            pe.wait_ge(m["masked"], 2 * q + 2)
                            if at(i, s, 4, 3) is not None:
                                pe.wait_ge(m["summed"], 2 * at(i, s, 4, 3) + 2)
                            for u in range(G8):
                                o = looked_up[r % 2][:, u * 32:(u + 1) * 32]
                                pe.matmul(o, lowt(r)[:, u * P:(u + 1) * P], seen(r)[:, u * 32:(u + 1) * 32], start=True, stop=False)
                                last = pe.matmul(o, same(r)[:, u * P:(u + 1) * P], high(r)[:, u * 32:(u + 1) * 32], start=False, stop=True)
                            last.then_inc(m["looked"], 1)
                    loop(pe, GROUPS, step, 4, drain=1)

                @block.scalar
                def _(act):
                    def step(i, s):
                        g = at(i, s, 4)
                        act.wait_ge(m["turned"], g + 1)
                        if at(i, s, 4, 2) is not None:
                            act.wait_ge(m["looked"], at(i, s, 4, 2) + 1)
                        if at(i, s, 4, 4) is not None:
                            act.wait_ge(kept[s], i * 32)
                        nc.scalar.copy(lowt_b(s), turn).then_inc(m["lifted"], 1)
                        nc.scalar.copy(lowt(s), turn).then_inc(m["lifted"], 1)
                    loop(act, GROUPS, step, 4)

                @block.sync
                def _(sp):
                    def step(i, s):
                        g = at(i, s, 4)
                        sp.wait_ge(m["lifted"], 2 * g + 2)
                        sp.dma_start(low_turned[:, bass.ds(g * G8 * P, G8 * P)], lowt_b(s)).then_inc(kept[s], 16)
                        sp.dma_start(high_kept[:, bass.ds(g * G8 * 32, G8 * 32)], high(s)).then_inc(kept[s], 16)
                    loop(sp, GROUPS, step, 4)
                    for n in range(4):
                        sp.wait_ge(kept[n], len(range(n, GROUPS, 4)) * 32)

        sent_tiles = [0]
        SCATTER_SEMS = ("sc_staged", "sc_go", "sc_sent0", "sc_sent1")

        def scatters(block, m, groups):
            if not groups:
                return
            first = sent_tiles[0]
            sent_tiles[0] += groups * G8
            sent = (m["sc_sent0"], m["sc_sent1"])
            to = lambda s: stage_i[:, s * G8:(s + 1) * G8]
            what = lambda s: onehot[:, s * 2 * G8:(s + 1) * 2 * G8].bitcast(I32)

            @block.gpsimd
            def _(g):
                def step(i, s):
                    q = at(i, s, 2)
                    if at(i, s, 2, 2) is not None:
                        g.wait_ge(sent[s], i * 16 * G8)
                        g.sem_inc(m["sc_go"], 1)
                    g.tensor_copy(to(s), place[:, bass.ds(q * G8 + first, G8)]).then_inc(m["sc_staged"], 1)
                    g.tensor_copy(what(s), pair[:, bass.ds(q * (2 * G8) + 2 * first, 2 * G8)]).then_inc(m["sc_staged"], 1)
                    g.wait_ge(m["sc_staged"], 2 * q + 2)
                    g.sem_inc(m["sc_go"], 1)
                    for n in range(G8):
                        g.indirect_dma_start(out=pair_list[:, :],
                                             out_offset=bass.IndirectOffsetOnAxis(ap=to(s)[:, n:n + 1], axis=0),
                                             in_=what(s)[:, 2 * n:2 * n + 2], in_offset=None).then_inc(sent[s], 16)
                loop(g, groups, step, 2)
                g.wait_ge(sent[0], (groups + 1) // 2 * 16 * G8)
                g.wait_ge(sent[1], groups // 2 * 16 * G8)

        def store_table(src_tile):
            with phase("stored") as (block, m):
                @block.sync
                def _(sp):
                    sp.dma_start(table_v, blocks(src_tile)).then_inc(m["stored"], 16)
                    sp.wait_ge(m["stored"], 16)

        def layernorm(src, dst, affine=None, add_to=None):
            half = BLOCKS // 2
            stats = wrows[:, 0:6 * BLOCKS].rearrange("p (b s) -> p b s", s=6)
            mean, diff, var, rstd, shift = (small[:, n * 32:n * 32 + BLOCKS] for n in range(5))
            shape = [P, BLOCKS, F]
            blk = lambda t, b: t[:, b * F:(b + 1) * F]
            with phase("rows_in", "vec", "counted", "ready", "rooted", "finished") as (block, m):
                rows_in, vec = m["rows_in"], m["vec"]

                @block.sync
                def _(sp):
                    if affine:
                        sp.dma_start(row_a[:, :], bc(io[affine[0]].rearrange("(o f) -> o f", o=1), [P, F])).then_inc(rows_in, 16)
                        sp.dma_start(row_b[:, :], bc(io[affine[1]].rearrange("(o f) -> o f", o=1), [P, F])).then_inc(rows_in, 16)

                @block.vector
                def _(v):
                    do = in_turn(v, vec)
                    for b in range(BLOCKS):
                        v.bn_stats(stats[:, b, :], blk(src, b)).then_inc(m["counted"], 1)
                    v.wait_ge(m["counted"], BLOCKS)
                    do(v.tensor_tensor(mean, stats[:, :, 1], stats[:, :, 4], ALU.add))
                    do(v.tensor_tensor(diff, stats[:, :, 1], stats[:, :, 4], ALU.subtract))
                    do(v.tensor_tensor(var, stats[:, :, 2], stats[:, :, 5], ALU.add))
                    do(v.tensor_scalar(mean, mean, 0.5, None, ALU.mult))
                    do(v.tensor_scalar(var, var, 1.0 / F, 1e-5, ALU.mult, ALU.add))
                    do(v.scalar_tensor_tensor(diff, diff, 0.25, diff, ALU.mult, ALU.mult))
                    do(v.tensor_tensor(var, var, diff, ALU.add))
                    v.sem_inc(m["ready"], 1)
                    v.wait_ge(m["rooted"], 1)
                    do(v.reciprocal(rstd, rstd))
                    do(v.scalar_tensor_tensor(shift, mean, -1.0, rstd, ALU.mult, ALU.mult))
                    v.sem_inc(m["ready"], 1)
                    for b in range(0 if affine else half, BLOCKS):
                        v.tensor_scalar(blk(dst, b), blk(src, b), rstd[:, b:b + 1], shift[:, b:b + 1], ALU.mult, ALU.add).then_inc(m["finished"], 1)
                    if affine:
                        d3 = blocks(dst)
                        v.wait_ge(rows_in, 32)
                        v.wait_ge(m["finished"], BLOCKS)
                        do(v.tensor_tensor(d3, d3, bc(row_a[:, :].unsqueeze(1), shape), ALU.mult))
                        do(v.tensor_tensor(d3, d3, bc(row_b[:, :].unsqueeze(1), shape), ALU.add))
                        if add_to is not None:
                            do(v.tensor_tensor(add_to[:, :], add_to[:, :], dst[:, :], ALU.add))
                    else:
                        v.wait_ge(m["finished"], BLOCKS - half)
                        do(v.tensor_scalar(dst[:, half * F:], dst[:, half * F:], 0.0, None, ALU.max))

                @block.scalar
                def _(act):
                    act.wait_ge(m["ready"], 1)
                    nc.scalar.activation(rstd, var, ACT.Sqrt).then_inc(m["rooted"], 1)
                    if not affine:
                        act.wait_ge(m["ready"], 2)
                        for b in range(half):
                            nc.scalar.activation(blk(dst, b), blk(src, b), ACT.Relu, bias=shift[:, b:b + 1], scale=rstd[:, b:b + 1])

        def load_weights(name, turned):
            w = io[name]
            ins = w.shape[1] if turned else w.shape[0]
            n = ins // P
            raw = x_eng[:, 0:2 * ins]
            with phase("w_in", "turned", "copied") as (block, m):
                w_in, turned_s, copied = m["w_in"], m["turned"], m["copied"]

                @block.sync
                def _(sp):
                    if turned:
                        sp.dma_start(raw.rearrange("p (o i) -> p o i", o=2), w.rearrange("(o p) i -> p o i", p=P)).then_inc(w_in, 16)
                    else:
                        sp.dma_start(weights[:, 0:n * F].rearrange("p (c o) -> p c o", c=n),
                                     w.rearrange("(c p) o -> p c o", p=P)).then_inc(w_in, 16)
                    sp.wait_ge(w_in, 16)

                if turned:
                    @block.tensor
                    def _(pe):
                        pe.wait_ge(w_in, 16)
                        for c in range(n):
                            for o in range(2):
                                last = pe.transpose(psum[c][:, o * P:(o + 1) * P], raw[:, o * ins + c * P:o * ins + (c + 1) * P],
                                                    ident[:, :])
                            last.then_inc(turned_s, 1)

                    @block.vector
                    def _(v):
                        for c in range(n):
                            v.wait_ge(turned_s, c + 1)
                            v.tensor_copy(weights[:, c * F:(c + 1) * F], psum[c][:, 0:F]).then_inc(copied, 1)

        def linear(inputs, dst, bias=None, relu=False, plus=None, to_table=False, send=0):
            n = 2 * len(inputs)
            lhs = lambda b: x_eng[:, b % 4 * 512:b % 4 * 512 + n * P]
            biased = lambda b: ring[:, b % 4 * F:(b % 4 + 1) * F]
            turn, res = (lambda b: psum[b % 4]), (lambda b: psum[4 + b % 4][:, 0:F])
            part = lambda t, b, c: t[:, b * (W8 if t is agg else F) + c * P:b * (W8 if t is agg else F) + (c + 1) * P]
            tab5 = table.rearrange("(g b p) f -> g p b f", b=5, p=P)
            with phase("row_in", "turned", "copied", "multiplied", "taken", "finished", "stored", *SCATTER_SEMS) as (block, m):
                scatters(block, m, send)
                row_in, turned, copied = (m[x] for x in ("row_in", "turned", "copied"))
                multiplied, taken, finished, stored = (m[x] for x in ("multiplied", "taken", "finished", "stored"))

                @block.tensor
                def _(pe):
                    for b in range(BLOCKS + 2):
                        if b < BLOCKS:
                            if b >= 4:
                                pe.wait_ge(copied, b - 3)
                            for c in range(n):
                                last = pe.transpose(turn(b)[:, c * P:(c + 1) * P], part(inputs[c // 2], b, c % 2), ident[:, :])
                            last.then_inc(turned, 1)
                        q = b - 2
                        if q >= 0:
                            pe.wait_ge(copied, q + 1)
                            if q >= 4:
                                pe.wait_ge(taken, q - 3)
                            for c in range(n):
                                last = pe.matmul(res(q), lhs(q)[:, c * P:(c + 1) * P], weights[:, c * F:(c + 1) * F],
                                                 start=(c == 0), stop=(c == n - 1))
                            last.then_inc(multiplied, 1)

                @block.scalar
                def _(act):
                    for b in range(BLOCKS):
                        act.wait_ge(turned, b + 1)
                        if b >= 4:
                            act.wait_ge(multiplied, b - 3)
                        nc.scalar.copy(lhs(b), turn(b)[:, 0:n * P]).then_inc(copied, 1)

                @block.vector
                def _(v):
                    if bias:
                        v.wait_ge(row_in, 16)
                    for b in range(BLOCKS):
                        v.wait_ge(multiplied, b + 1)
                        o = dst[:, b * F:(b + 1) * F]
                        if not bias:
                            v.tensor_copy(o, res(b)).then_inc(taken, 1)
                            continue
                        if b >= 4:
                            v.wait_ge(finished, b - 3)
                        v.tensor_tensor(biased(b), res(b), row_a[:, :], ALU.add).then_inc(taken, 1)
                        v.wait_ge(taken, b + 1)
                        if plus is not None:
                            v.scalar_tensor_tensor(o, biased(b), 0.0, plus[:, b * F:(b + 1) * F], ALU.max, ALU.add).then_inc(finished, 1)
                        else:
                            v.tensor_scalar(o, biased(b), 0.0, None, ALU.max).then_inc(finished, 1)

                @block.sync
                def _(sp):
                    if bias:
                        sp.dma_start(row_a[:, :], bc(io[bias].rearrange("(o f) -> o f", o=1), [P, F])).then_inc(row_in, 16)
                        sp.wait_ge(row_in, 16)
                    if to_table:
                        for g in range(BLOCKS // 5):
                            sp.wait_ge(finished if bias else taken, (g + 1) * 5)
                            sp.dma_start(tab5[g], blocks(dst)[:, g * 5:(g + 1) * 5, :]).then_inc(stored, 16)
                        sp.wait_ge(stored, 16 * (BLOCKS // 5))

        def gathers(g, rows, src, dest, m, freed):
            half = UNROLL // 2
            def round_(i, r):
                n = i * 2 + r
                for h in range(2):
                    if not isinstance(n, int) or n > 0:
                        g.wait_ge(freed, n * UNROLL + h * half - half)
                        g.sem_inc(m["go"], 1)
                    if h == 0:
                        g.tensor_copy(stage_i[:, r * UNROLL:(r + 1) * UNROLL], rows[:, bass.ds(n * UNROLL, UNROLL)]).then_inc(m["staged"], 1)
                        g.wait_ge(m["staged"], n + 1)
                        g.sem_inc(m["go"], 1)
                    for u in range(h * half, (h + 1) * half):
                        at_u = r * UNROLL + u
                        g.indirect_dma_start(out=dest(u), out_offset=None, in_=src,
                                             in_offset=bass.IndirectOffsetOnAxis(ap=stage_i[:, at_u:at_u + 1], axis=0)).then_inc(m[f"row{u}"], 16)
            round_(0, 0)
            round_(0, 1)
            with g.Fori(1, STEPS // UNROLL // 2) as i:
                round_(i, 0)
                round_(i, 1)

        ROW_SEMS = [f"row{n}" for n in range(UNROLL)]
        slot = lambda s: ring[:, (s % UNROLL) * F:(s % UNROLL + 1) * F]
        oneh = lambda s: onehot[:, (s % 4) * P:(s % 4 + 1) * P]

        def stage_nodes(v, m, nodes, i, s):
            if s == 0:
                if not isinstance(i, int):
                    v.wait_ge(m["made"], i * UNROLL)
                v.tensor_copy(node_st[:, :], nodes[:, bass.ds(i * UNROLL, UNROLL)]).then_inc(m["nodes"], 1)
                v.wait_ge(m["nodes"], i + 1)

        def add_to_block(v, m, block_tab, i, s, blk, width, lag):
            q = at(i, s, UNROLL, lag)
            if q is None:
                return
            v.wait_ge(m["brought"], q + 1)
            v.wait_ge(m["added"], q + 1)
            o = agg[:, bass.ds(blk * W8, width)]
            v.tensor_tensor(o, o, psum[(s - lag) % 4][:, 0:width], ALU.add).then_inc(m["added"], 1)

        def load_blocks(v, block_tab, i, lag):
            _, vals = nc.values_load_multi_w_load_instructions(
                block_tab[0:1, bass.ds(i * UNROLL + LAG - lag, UNROLL)], engines=(DVE,), min_val=0, max_val=BLOCKS - 1,
                skip_runtime_bounds_check_because="counted from the steps")
            return vals

        def block_loop(v, block_tab, lag, step):
            vals = load_blocks(v, block_tab, 0, lag)
            for s in range(UNROLL):
                step(0, s, vals[s])
            with v.Fori(1, STEPS // UNROLL) as i:
                vals = load_blocks(v, block_tab, i, lag)
                for s in range(UNROLL):
                    step(i, s, vals[s])
            n = STEPS // UNROLL
            vals = load_blocks(v, block_tab, n, lag)
            for s in range(lag):
                step(n, s, vals[s])

        def sum_pass(by_dst, weighted):
            node_k, row_k, block_k = (node_d, row_d, block_d) if by_dst else (node_s, row_s, block_s)
            width = W8 if weighted else F
            lag = LAG
            wrow = lambda s: wrows[:, (s % 4) * W8:(s % 4 + 1) * W8]
            with phase("freed", "go", "staged", "nodes", "made", "weighed", "brought", "added", *ROW_SEMS) as (block, m):

                @block.gpsimd
                def _(g):
                    gathers(g, row_k, table[:, :], slot, m, m["freed"] if weighted else m["brought"])

                @block.vector
                def _(v):
                    v.memset(agg[:, :], 0.0).then_inc(m["added"], 1)
                    def step(i, s, blk):
                        k = i * UNROLL + s
                        if not (isinstance(k, int) and k >= STEPS):
                            if at(i, s, UNROLL, 4) is not None:
                                v.wait_ge(m["brought"], at(i, s, UNROLL, 4) + 1)
                            stage_nodes(v, m, node_k, i, s)
                            v.tensor_scalar(oneh(s), iota_f[:, :], node_st[:, s:s + 1], None, ALU.is_equal).then_inc(m["made"], 1)
                            if weighted:
                                w4 = w_edge[:, bass.ds(k * HEADS, HEADS)]
                                v.wait_ge(m[f"row{s}"], i * 16 + 16)
                                v.tensor_tensor(wrow(s)[:, 0:F].rearrange("p (h c) -> p h c", h=HEADS),
                                                slot(s).rearrange("p (h c) -> p h c", h=HEADS),
                                                bc(w4.unsqueeze(2), [P, HEADS, C]), ALU.mult).then_inc(m["freed"], 1)
                                v.tensor_copy(wrow(s)[:, F:W8], w4).then_inc(m["weighed"], 1)
                        add_to_block(v, m, block_k, i, s, blk, width, lag)
                    block_loop(v, block_k, lag, step)

                @block.tensor
                def _(pe):
                    def step(i, s):
                        k = i * UNROLL + s
                        pe.wait_ge(m["made"], k + 1)
                        if at(i, s, UNROLL, 4) is not None:
                            pe.wait_ge(m["added"], at(i, s, UNROLL, 4) + 2)
                        if weighted:
                            pe.wait_ge(m["freed"], k + 1)
                            pe.wait_ge(m["weighed"], k + 1)
                            pe.matmul(psum[s % 4][:, 0:W8], oneh(s), wrow(s), start=True, stop=True).then_inc(m["brought"], 1)
                        else:
                            pe.wait_ge(m[f"row{s}"], i * 16 + 16)
                            pe.matmul(psum[s % 4][:, 0:F], oneh(s), slot(s), start=True, stop=True).then_inc(m["brought"], 1)
                    loop(pe, STEPS, step, UNROLL)

        def max_pass():
            lag = LAG
            run = lambda s, h: x_eng[:, (s % 4) * F + h * P:(s % 4) * F + (h + 1) * P]
            back = lambda s: wrows[:, (s % 2) * F:(s % 2 + 1) * F]
            mask = lambda s: small[:, (s % 2) * P:(s % 2 + 1) * P]
            picks = lambda s, n=1: x_eng[:, 1024 + (s % 8) * P:1024 + (s % 8 + n) * P]
            tg = lambda s: psum[4 + s % 2]
            tb = lambda s: psum[6 + s % 2]
            with phase("go", "staged", "marked", "made", "turned", "masked", "scanned", "returned", "lifted",
                       "brought", "added", *ROW_SEMS) as (block, m):

                @block.gpsimd
                def _(g):
                    gathers(g, row_d, table[:, :], slot, m, m["turned"])

                @block.tensor
                def _(pe):
                    def step(i, s):
                        k = i * UNROLL + s
                        if not (isinstance(k, int) and k >= STEPS):
                            if s == 0:
                                pe.wait_ge(m["marked"], i + 1)
                            pe.wait_ge(m[f"row{s}"], i * 16 + 16)
                            if at(i, s, UNROLL, 2) is not None:
                                pe.wait_ge(m["scanned"], 2 * at(i, s, UNROLL, 2) + 2)
                            for h in range(2):
                                pe.transpose(tg(s)[:, h * P:(h + 1) * P], slot(s)[:, h * P:(h + 1) * P], ident[:, :])
                            pe.matmul(tg(s)[:, F:F + P], bc(mark[:, s:s + 1], [P, P]), ident_b[:, :], start=True, stop=True,
                                      skip_group_check=True).then_inc(m["turned"], 1)
                        q = at(i, s, UNROLL, 2)
                        if live(q, STEPS):
                            pe.wait_ge(m["scanned"], 2 * q + 2)
                            if at(i, s, UNROLL, 4) is not None:
                                pe.wait_ge(m["lifted"], at(i, s, UNROLL, 4) + 1)
                            for h in range(2):
                                last = pe.transpose(tb(s)[:, h * P:(h + 1) * P], run(s - 2, h), ident[:, :])
                            last.then_inc(m["returned"], 1)
                        q = at(i, s, UNROLL, 3)
                        if q is not None:
                            pe.wait_ge(m["made"], i * 4 + (s - 3) // 4 + 1)
                            pe.wait_ge(m["lifted"], q + 1)
                            if at(i, s, UNROLL, 7) is not None:
                                pe.wait_ge(m["added"], at(i, s, UNROLL, 7) + 3)
                            pe.matmul(psum[(s - 3) % 4][:, 0:F], picks(s - 3), back(s - 3), start=True, stop=True).then_inc(m["brought"], 1)
                    loop(pe, STEPS, step, UNROLL, drain=3)

                @block.scalar
                def _(act):
                    def step(i, s):
                        k = i * UNROLL + s
                        if not (isinstance(k, int) and k >= STEPS):
                            if s == 0:
                                if not isinstance(i, int):
                                    act.wait_ge(m["turned"], i * UNROLL)
                                    act.sem_inc(m["go"], 1)
                                nc.scalar.copy(mark[:, :], start_d[:, bass.ds(k, UNROLL)]).then_inc(m["marked"], 1)
                            act.wait_ge(m["turned"], k + 1)
                            nc.scalar.copy(mask(s), tg(s)[:, F:F + P]).then_inc(m["masked"], 1)
                        q = at(i, s, UNROLL, 2)
                        if q is not None:
                            act.wait_ge(m["returned"], q + 1)
                            if at(i, s, UNROLL, 4) is not None:
                                act.wait_ge(m["brought"], at(i, s, UNROLL, 4) + 1)
                            nc.scalar.copy(back(s), tb(s)[:, 0:F]).then_inc(m["lifted"], 1)
                    loop(act, STEPS, step, UNROLL, drain=2)

                @block.vector
                def _(v):
                    v.memset(agg[:, :], 0.0).then_inc(m["added"], 1)
                    v.memset(x_eng[:, 0:4 * F], -BIG).then_inc(m["added"], 1)
                    v.wait_ge(m["added"], 2)
                    def step(i, s, blk):
                        k = i * UNROLL + s
                        if not (isinstance(k, int) and k >= STEPS):
                            if s % 4 == 0:
                                if at(i, s, UNROLL, 5) is not None:
                                    v.wait_ge(m["brought"], at(i, s, UNROLL, 5) + 1)
                                    v.wait_ge(m["made"], i * 4 + s // 4 - 1)
                                v.tensor_tensor(picks(s, 4).rearrange("p (s e) -> p s e", e=P), bc(iota_f[:, :].unsqueeze(1), [P, 4, P]),
                                                bc(last_d[:, bass.ds(k, 4)].unsqueeze(2), [P, 4, P]), ALU.is_equal).then_inc(m["made"], 1)
                            v.wait_ge(m["masked"], k + 1)
                            if at(i, s, UNROLL, 4) is not None:
                                v.wait_ge(m["returned"], at(i, s, UNROLL, 4) + 1)
                            if at(i, s, UNROLL, 1) is not None:
                                v.wait_ge(m["scanned"], 2 * at(i, s, UNROLL, 1) + 2)
                            for h in range(2):
                                v.tensor_tensor_scan(run(s, h), mask(s), tg(s)[:, h * P:(h + 1) * P],
                                                     run(s - 1, h)[:, P - 1:P], ALU.add, ALU.max).then_inc(m["scanned"], 1)
                        q = at(i, s, UNROLL, lag)
                        if q is None:
                            return
                        v.wait_ge(m["brought"], q + 1)
                        v.wait_ge(m["added"], q + 2)
                        o = agg[:, bass.ds(blk * W8, F)]
                        v.tensor_tensor(o, o, psum[(s - lag) % 4][:, 0:F], ALU.add).then_inc(m["added"], 1)
                    block_loop(v, block_d, lag, step)


        def in_turn(eng, sem):
            n = [0]

            def do(inst):
                inst.then_inc(sem, 1)
                n[0] += 1
                eng.wait_ge(sem, n[0])
            return do

        row3 = lambda t, w: t.rearrange("t (j e w) -> t j e w", j=CHUNKS, w=w)
        f_gather = agg[:, 0:2048]
        f_row = agg[:, 2048:4096]
        s_row = agg[:, 4096:6144]
        g_row = x_eng[:, 0:4096]
        g_full = ring[:, 0:4096]
        sm_node = small[:, 0:BLOCKS * HEADS]

        def segment_masks():
            any_r = small[:, 0:4]
            st = start_r[:, :].rearrange("t (j e) -> t j e", j=CHUNKS)
            with phase("vec", "turned") as (block, m):
                @block.vector
                def _(v):
                    do = in_turn(v, m["vec"])
                    do(v.tensor_reduce(any_r, st, AX.X, ALU.max))
                    do(v.tensor_scalar(first_keep[:, :], st[:, :, 0], -1.0, 1.0, ALU.mult, ALU.add))
                    do(v.tensor_scalar(first_open[:, :], st[:, :, 0], -BIG, None, ALU.mult))
                    do(v.tensor_scalar(keep_r[:, :], start_r[:, :], -1.0, 1.0, ALU.mult, ALU.add))
                    do(v.tensor_scalar(open_r[:, :], start_r[:, :], -BIG, None, ALU.mult))
                    do(v.memset(keep_r[:, :].rearrange("t (j e) -> t j e", j=CHUNKS)[:, :, 0], 0.0))
                    do(v.memset(open_r[:, :].rearrange("t (j e) -> t j e", j=CHUNKS)[:, :, 0], -BIG))
                    do(v.tensor_copy(small[:, 8:40].rearrange("t (j r) -> t j r", j=CHUNKS),
                                     bc(any_r.unsqueeze(2), [P, CHUNKS, 8])))
                    v.wait_ge(m["turned"], 1)
                    do(v.tensor_scalar(chain_keep[:, :], psum[0][0:8, :], -1.0, 1.0, ALU.mult, ALU.add))
                    do(v.tensor_scalar(chain_open[:, :], psum[0][0:8, :], -BIG, None, ALU.mult))

                @block.tensor
                def _(pe):
                    pe.wait_ge(m["vec"], 8)
                    for j in range(CHUNKS):
                        last = pe.transpose(psum[0][0:8, j * P:(j + 1) * P], small[:, 8 + 8 * j:16 + 8 * j], ident[:, :])
                    last.then_inc(m["turned"], 1)

        def segment_scan(v, pe, data, result, planes, maximum, m):
            mask, chain, first = (open_r, chain_open, first_open) if maximum else (keep_r, chain_keep, first_keep)
            ops = (ALU.add, ALU.max) if maximum else (ALU.mult, ALU.add)
            empty = -BIG if maximum else 0.0
            d4, r4 = row3(data, planes), row3(result, planes)
            d3 = data.rearrange("t (s w) -> t s w", w=planes)
            r3 = result.rearrange("t (s w) -> t s w", w=planes)
            patch = small[:, 128:128 + CHUNKS * planes].rearrange("t (j w) -> t j w", w=planes)

            def vector_part(do):
                def scans():
                    for w in range(planes):
                        do(v.tensor_tensor_scan(r3[:, :, w], mask[:, :], d3[:, :, w], empty, *ops))
                scans()
                v.sem_inc(m["scanned"], 1)
                v.wait_ge(m["turned"], 1)
                do(v.memset(carry[0:planes, 0:1], empty))
                do(v.tensor_tensor_scan(carry[0:planes, 1:], chain[0:planes, :], psum[4][0:planes, :], empty, *ops))
                v.sem_inc(m["scanned"], 1)
                v.wait_ge(m["turned"], 2)
                back = psum[5][:, 0:CHUNKS * planes].rearrange("t (j w) -> t j w", w=planes)
                do(v.tensor_tensor(patch, back, bc(first[:, :].unsqueeze(2), [P, CHUNKS, planes]), ops[0]))
                do(v.tensor_tensor(d4[:, :, 0, :], d4[:, :, 0, :], patch, ops[1]))
                scans()

            def tensor_part():
                pe.wait_ge(m["scanned"], 1)
                for j in range(CHUNKS):
                    last = pe.transpose(psum[4][0:planes, j * P:(j + 1) * P], r4[:, j, P - 1, :], ident[:, :])
                last.then_inc(m["turned"], 1)
                pe.wait_ge(m["scanned"], 2)
                for j in range(CHUNKS):
                    last = pe.transpose(psum[5][:, j * planes:(j + 1) * planes], carry[0:planes, j * P:(j + 1) * P],
                                        ident[0:planes, 0:planes])
                last.then_inc(m["turned"], 1)
            return vector_part, tensor_part

        def node_scores(global_softmax, a_src, a_dst, h):
            prod = agg[:, 0:BLOCKS * F]
            with phase("rows_in", "vec") as (block, m):
                rows_in, vec = m["rows_in"], m["vec"]

                @block.sync
                def _(sp):
                    for row, a in ((row_a, a_src), (row_b, a_dst)):
                        sp.dma_start(row[:, :].rearrange("p (h c) -> p h c", h=HEADS), bc(a, [P, HEADS, C])).then_inc(rows_in, 16)

                @block.vector
                def _(v):
                    do = in_turn(v, vec)
                    pad_first = NODES - (BLOCKS - 1) * P
                    src = h
                    do(v.memset(gm_node[:, :], 0.0))
                    if global_softmax:
                        do(v.scalar_tensor_tensor(act_a[:, :], h[:, :], 0.2, h[:, :], ALU.mult, ALU.max))
                        src = act_a
                    v.wait_ge(rows_in, 32)
                    for row, o in ((row_a, f3), (row_b, gm4[:, :, 0, :])):
                        do(v.tensor_tensor(prod.rearrange("p (b f) -> p b f", f=F), blocks(src),
                                           bc(row[:, :].unsqueeze(1), [P, BLOCKS, F]), ALU.mult))
                        do(v.tensor_reduce(o, prod.rearrange("p (b h c) -> p b h c", h=HEADS, c=C), AX.X, ALU.add))
                    if global_softmax:
                        do(v.tensor_scalar(small[:, 0:1], iota_p[:, :], float(pad_first), -1e30, ALU.is_ge, ALU.mult))
                        do(v.tensor_scalar(gm4[:, BLOCKS - 1, 0, :], gm4[:, BLOCKS - 1, 0, :], small[:, 0:1], None, ALU.add))

        def look_up_scores(send):
            low = lambda s: ring[:, s % 4 * 512:(s % 4 + 1) * 512].bitcast(BF16)
            high = lambda s: ring[:, 2048 + s % 4 * 128:2176 + s % 4 * 128].bitcast(BF16)
            prod = lambda s, n: x_eng[:, (s % 2 * 2 + n) * 400:(s % 2 * 2 + n + 1) * 400].rearrange(
                "p (t b h) -> p t b h", t=4, h=HEADS)
            BH = BLOCKS * HEADS
            part = [wrows[:, n * 64:n * 64 + 50].bitcast(BF16) for n in range(3)]
            rest = [wrows[:, 256 + n * 128:256 + n * 128 + BH] for n in range(2)]
            with phase("split", "came0", "came1", "came2", "came3", "looked", "masked", "summed", "cleared",
                       *SCATTER_SEMS) as (block, m):
                scatters(block, m, send)
                came = [m[f"came{n}"] for n in range(4)]

                @block.sync
                def _(sp):
                    def step(i, s):
                        g = at(i, s, 4)
                        if at(i, s, 4, 4) is not None:
                            sp.wait_ge(m["looked"], at(i, s, 4, 4) + 1)
                            sp.wait_ge(m["masked"], 2 * at(i, s, 4, 4) + 2)
                        sp.dma_start(low(s), low_turned[:, bass.ds(g * G8 * P, G8 * P)]).then_inc(came[s], 16)
                        sp.dma_start(high(s), high_kept[:, bass.ds(g * G8 * 32, G8 * 32)]).then_inc(came[s], 16)
                    loop(sp, GROUPS, step, 4)

                @block.vector
                def _(v):
                    v.memset(f_gather[:, TILES * HEADS:], 0.0).then_inc(m["cleared"], 1)
                    do = in_turn(v, m["split"])
                    do(v.tensor_copy(part[0], f_node[:, :]))
                    do(v.tensor_tensor(rest[0], f_node[:, :], part[0], ALU.subtract))
                    do(v.tensor_copy(part[1], rest[0]))
                    do(v.tensor_tensor(rest[1], rest[0], part[1], ALU.subtract))
                    do(v.tensor_copy(part[2], rest[1]))
                    def step(i, s):
                        q = at(i, s, 4)
                        v.wait_ge(m["looked"], q + 1)
                        if at(i, s, 4, 2) is not None:
                            v.wait_ge(m["summed"], 2 * at(i, s, 4, 2) + 2)
                        for n in range(2):
                            h4 = high(s)[:, n * 128:(n + 1) * 128].rearrange("p (t b) -> p t b", b=32)[:, :, 0:BLOCKS]
                            v.tensor_tensor(prod(s, n), psum[2 * (s % 2) + n][:, 0:4 * BH].rearrange("p (t b h) -> p t b h", t=4, h=HEADS),
                                            bc(h4.unsqueeze(3), [P, 4, BLOCKS, HEADS]), ALU.mult).then_inc(m["masked"], 1)
                        for n in range(2):
                            v.wait_ge(m["masked"], 2 * q + 1 + n)
                            o = f_gather[:, bass.ds(q * G8 * HEADS + n * 4 * HEADS, 4 * HEADS)].rearrange("p (t h) -> p t h", h=HEADS)
                            v.tensor_reduce(o, prod(s, n).rearrange("p t b h -> p t h b"), AX.X, ALU.add).then_inc(m["summed"], 1)
                    loop(v, GROUPS, step, 4)

                @block.tensor
                def _(pe):
                    pe.wait_ge(m["split"], 5)
                    def step(i, s):
                        pe.wait_ge(came[s], i * 32 + 32)
                        if at(i, s, 4, 2) is not None:
                            pe.wait_ge(m["masked"], 2 * at(i, s, 4, 2) + 2)
                        for u in range(G8):
                            o = psum[2 * (s % 2) + u // 4][:, u % 4 * BH:(u % 4 + 1) * BH]
                            for n in range(3):
                                last = pe.matmul(o, low(s)[:, u * P:(u + 1) * P], part[n], start=(n == 0), stop=(n == 2))
                        last.then_inc(m["looked"], 1)
                    loop(pe, GROUPS, step, 4)

        def segment_maxima():
            saved = small[:, 200:216].rearrange("t (j w) -> t j w", w=HEADS)
            with phase("vec", "f_turned", "scanned", "turned", "stored", "read", "cleared") as (block, m):
                fr = f_row.rearrange("t (s w) -> t s w", w=HEADS)
                fr4 = row3(f_row, HEADS)
                parts = {}

                @block.vector
                def _(v):
                    do = in_turn(v, m["vec"])
                    v.wait_ge(m["f_turned"], 1)
                    for h in range(HEADS):
                        do(v.tensor_copy(fr[:, :, h], psum[h][:, :]))
                    do(v.tensor_copy(saved, fr4[:, :, 0, :]))
                    parts["v"], parts["pe"] = segment_scan(v, nc.tensor, f_row, s_row, HEADS, True, m)
                    parts["v"](do)
                    v.sem_inc(m["scanned"], 1)
                    do(v.tensor_copy(fr4[:, :, 0, :], saved))
                    do(v.memset(sm_node, -BIG))
                    v.sem_inc(m["cleared"], 1)

                @block.tensor
                def _(pe):
                    fg = f_gather.rearrange("e (t w) -> e t w", w=HEADS)
                    for h in range(HEADS):
                        for j in range(CHUNKS):
                            last = pe.transpose(psum[h][:, j * P:(j + 1) * P], fg[:, j * P:(j + 1) * P, h], ident[:, :])
                    last.then_inc(m["f_turned"], 1)
                    parts["pe"]()

                @block.sync
                def _(sp):
                    sp.wait_ge(m["scanned"], 3)
                    sp.dma_start(seg_maxima.rearrange("(j t e) h -> t j (e h)", j=CHUNKS, t=P),
                                 s_row.rearrange("t (j e) -> t j e", j=CHUNKS)).then_inc(m["stored"], 16)
                    sp.wait_ge(m["stored"], 16)

                @block.gpsimd
                def _(g):
                    g.wait_ge(m["stored"], 16)
                    g.wait_ge(m["cleared"], 1)
                    for b in range(BLOCKS):
                        g.indirect_dma_start(out=sm_node[:, b * HEADS:(b + 1) * HEADS], out_offset=None, in_=seg_maxima[:, :],
                                             in_offset=bass.IndirectOffsetOnAxis(ap=final_row[:, b:b + 1], axis=0),
                                             bounds_check=SLOTS - 1, oob_is_err=False).then_inc(m["read"], 16)
                    g.wait_ge(m["read"], 16 * BLOCKS)

        def node_shifts(global_softmax):
            sm3 = sm_node.rearrange("p (b h) -> p b h", h=HEADS)
            g3, m3 = gm4[:, :, 0, :], gm4[:, :, 1, :]
            ws3 = w_self[:, :].rearrange("p (b h) -> p b h", h=HEADS)
            top = small[:, 224:228]
            dg = small[0:HEADS, 232:236]
            tmp = wrows[:, 0:BLOCKS * HEADS].rearrange("p (b h) -> p b h", h=HEADS)
            with phase("vec", "top", "turned", "exped", "ready", "sent") as (block, m):
                @block.vector
                def _(v):
                    do = in_turn(v, m["vec"])
                    do(v.tensor_tensor(sm3, sm3, f3, ALU.max))
                    do(v.tensor_tensor(sm3, sm3, g3, ALU.add))
                    if global_softmax:
                        do(v.tensor_reduce(top, sm_node.rearrange("p (b h) -> p h b", h=HEADS), AX.X, ALU.max))
                        v.sem_inc(m["top"], 1)
                        v.wait_ge(m["turned"], 1)
                        do(v.tensor_reduce(small[0:HEADS, 228:229], psum[0][0:HEADS, 0:P], AX.X, ALU.max))
                        do(v.tensor_scalar(dg, ident[0:HEADS, 0:HEADS], small[0:HEADS, 228:229], None, ALU.mult))
                        v.sem_inc(m["top"], 1)
                        v.wait_ge(m["turned"], 2)
                        do(v.tensor_copy(top, psum[1][:, 0:HEADS]))
                        do(v.tensor_tensor(g3, g3, bc(top.unsqueeze(1), [P, BLOCKS, HEADS]), ALU.subtract))
                        do(v.tensor_tensor(tmp, f3, g3, ALU.add))
                    else:
                        do(v.scalar_tensor_tensor(m3, sm3, 0.2, sm3, ALU.mult, ALU.max))
                        do(v.tensor_tensor(sm3, f3, g3, ALU.add))
                        do(v.scalar_tensor_tensor(tmp, sm3, 0.2, sm3, ALU.mult, ALU.max))
                        do(v.tensor_tensor(tmp, tmp, m3, ALU.subtract))
                    v.sem_inc(m["ready"], 1)

                @block.scalar
                def _(act):
                    act.wait_ge(m["ready"], 1)
                    nc.scalar.activation(ws3, tmp, ACT.Exp).then_inc(m["exped"], 1)

                if global_softmax:
                    @block.tensor
                    def _(pe):
                        pe.wait_ge(m["top"], 1)
                        pe.transpose(psum[0][0:HEADS, 0:P], top, ident[:, :]).then_inc(m["turned"], 1)
                        pe.wait_ge(m["top"], 2)
                        pe.matmul(psum[1][:, 0:HEADS], ones[0:HEADS, :], dg, start=True, stop=True).then_inc(m["turned"], 1)

                @block.gpsimd
                def _(g):
                    g.wait_ge(m["ready"], 1)
                    for b in range(BLOCKS):
                        g.indirect_dma_start(out=seg_starts[:, :],
                                             out_offset=bass.IndirectOffsetOnAxis(ap=first_row[:, b:b + 1], axis=0),
                                             in_=gm_node[:, b * 2 * HEADS:(b + 1) * 2 * HEADS], in_offset=None,
                                             bounds_check=SLOTS - 1, oob_is_err=False).then_inc(m["sent"], 16)
                    g.wait_ge(m["sent"], 16 * BLOCKS)

        def edge_weights(global_softmax):
            gf = g_full.rearrange("t (s w) -> t s w", w=2 * HEADS)
            sr = s_row.rearrange("t (s w) -> t s w", w=HEADS)
            fr = f_row.rearrange("t (s w) -> t s w", w=HEADS)
            w3 = w_edge[:, :].rearrange("e (k h) -> e k h", h=HEADS)
            with phase("vec", "loaded", "scanned", "turned", "exped", "picked", "ready") as (block, m):
                parts = {}

                @block.sync
                def _(sp):
                    sp.dma_start(g_row.rearrange("t (j e) -> t j e", j=CHUNKS),
                                 seg_starts.rearrange("(j t e) c -> t j (e c)", j=CHUNKS, t=P)).then_inc(m["loaded"], 16)

                @block.vector
                def _(v):
                    do = in_turn(v, m["vec"])
                    v.wait_ge(m["loaded"], 16)
                    parts["v"], parts["pe"] = segment_scan(v, nc.tensor, g_row, g_full, 2 * HEADS, False, m)
                    parts["v"](do)
                    do(v.tensor_tensor(sr, fr, gf[:, :, 0:HEADS], ALU.add))
                    if not global_softmax:
                        do(v.scalar_tensor_tensor(sr, sr, 0.2, sr, ALU.mult, ALU.max))
                        do(v.tensor_tensor(sr, sr, gf[:, :, HEADS:], ALU.subtract))
                    v.sem_inc(m["ready"], 1)
                    v.wait_ge(m["picked"], 1)
                    for h in range(HEADS):
                        do(v.tensor_copy(w3[:, :, h], psum[h][:, 0:STEPS]))

                @block.scalar
                def _(act):
                    act.wait_ge(m["ready"], 1)
                    nc.scalar.activation(s_row, s_row, ACT.Exp).then_inc(m["exped"], 1)

                @block.tensor
                def _(pe):
                    parts["pe"]()
                    pe.wait_ge(m["exped"], 1)
                    for h in range(HEADS):
                        for j in range(CHUNKS):
                            last = pe.matmul(psum[h][:, 0:STEPS], sr[:, j * P:(j + 1) * P, h], of_step[:, j * STEPS:(j + 1) * STEPS],
                                             start=(j == 0), stop=(j == CHUNKS - 1))
                    last.then_inc(m["picked"], 1)

        def attention(global_softmax, a_src, a_dst, send):
            node_scores(global_softmax, a_src, a_dst, act_b)
            look_up_scores(send)
            segment_maxima()
            node_shifts(global_softmax)
            edge_weights(global_softmax)
            sum_pass(True, True)

        def attention_out(global_softmax, bias, last):
            ws3 = w_self[:, :].rearrange("p (b h) -> p b h", h=HEADS)
            den = small[:, 0:BLOCKS * HEADS].rearrange("p (b h) -> p b h", h=HEADS)
            total = small[:, 128:132]
            inv = small[:, 132:136]
            ha = heads(act_a)
            shape = [P, BLOCKS, HEADS, C]
            with phase("row_in", "vec", "summed", "ready", "finished") as (block, m):
                @block.sync
                def _(sp):
                    sp.dma_start(row_a[:, :], bc(io[bias].rearrange("(o f) -> o f", o=1), [P, F])).then_inc(m["row_in"], 16)

                @block.vector
                def _(v):
                    do = in_turn(v, m["vec"])
                    do(v.tensor_tensor(den, agg_den, ws3, ALU.add))
                    if global_softmax:
                        do(v.tensor_reduce(total, small[:, 0:BLOCKS * HEADS].rearrange("p (b h) -> p h b", h=HEADS), AX.X, ALU.add))
                        v.sem_inc(m["ready"], 1)
                    else:
                        do(v.reciprocal(small[:, 0:BLOCKS * HEADS], small[:, 0:BLOCKS * HEADS]))
                    do(v.tensor_tensor(ha, heads(act_b), bc(ws3.unsqueeze(3), shape), ALU.mult))
                    do(v.tensor_tensor(ha, ha, agg_h, ALU.add))
                    if global_softmax:
                        v.wait_ge(m["summed"], 1)
                        do(v.reciprocal(inv, psum[0][:, 0:HEADS]))
                        do(v.tensor_tensor(ha, ha, bc(inv.unsqueeze(1).unsqueeze(3), shape), ALU.mult))
                    else:
                        do(v.tensor_tensor(ha, ha, bc(den.unsqueeze(3), shape), ALU.mult))
                    v.wait_ge(m["row_in"], 16)
                    do(v.tensor_tensor(blocks(act_a), blocks(act_a), bc(row_a[:, :].unsqueeze(1), [P, BLOCKS, F]), ALU.add))
                    if not global_softmax:
                        v.sem_inc(m["ready"], 1)
                        v.wait_ge(m["finished"], 1)
                    if last:
                        do(v.tensor_tensor(x_res[:, :], x_res[:, :], act_a[:, :], ALU.add))

                if global_softmax:
                    @block.tensor
                    def _(pe):
                        pe.wait_ge(m["ready"], 1)
                        pe.matmul(psum[0][:, 0:HEADS], ones[:, :], total, start=True, stop=True).then_inc(m["summed"], 1)
                else:
                    @block.scalar
                    def _(act):
                        act.wait_ge(m["ready"], 1)
                        nc.scalar.activation(act_a[:, :], act_a[:, :], ACT.Gelu).then_inc(m["finished"], 1)

        def by_degree(deg, bias=None, plus=None):
            inv, has = small[:, 0:32], small[:, 32:64]
            shape = [P, BLOCKS, F]
            low = agg[:, 0:BLOCKS * F]
            tab5 = table.rearrange("(g b p) f -> g p b f", b=5, p=P)
            with phase("rows_in", "vec", "scaled", "stored") as (block, m):
                @block.sync
                def _(sp):
                    if bias:
                        sp.dma_start(row_a[:, :], bc(io[bias].rearrange("(o f) -> o f", o=1), [P, F])).then_inc(m["rows_in"], 16)
                        sp.dma_start(slope[:, :], bc(io["L3_gnn_a"].rearrange("(o f) -> o f", o=1), [P, 1])).then_inc(m["rows_in"], 16)
                        sp.wait_ge(m["rows_in"], 32)
                    else:
                        for g in range(BLOCKS // 5):
                            sp.wait_ge(m["scaled"], g + 1)
                            sp.dma_start(tab5[g], blocks(act_b)[:, g * 5:(g + 1) * 5, :]).then_inc(m["stored"], 16)
                        sp.wait_ge(m["stored"], 16 * (BLOCKS // 5))

                @block.vector
                def _(v):
                    do = in_turn(v, m["vec"])
                    do(v.tensor_scalar(has, deg[:, :], 0.0, None, ALU.is_gt))
                    do(v.tensor_scalar(inv, deg[:, :], 1.0, None, ALU.max))
                    do(v.reciprocal(inv, inv))
                    do(v.tensor_tensor(inv, inv, has, ALU.mult))
                    for g in range(0, BLOCKS, 5):
                        v.tensor_tensor(blocks(act_b)[:, g:g + 5, :], agg_f[:, g:g + 5, :],
                                        bc(inv[:, g:g + 5].unsqueeze(2), [P, 5, F]), ALU.mult).then_inc(m["scaled"], 1)
                    if bias:
                        v.wait_ge(m["scaled"], BLOCKS // 5)
                        v.wait_ge(m["rows_in"], 32)
                        do(v.tensor_tensor(blocks(act_b), blocks(act_b), bc(row_a[:, :].unsqueeze(1), shape), ALU.add))
                        if plus is not None:
                            do(v.tensor_tensor(act_b[:, :], act_b[:, :], plus[:, :], ALU.add))
                        do(v.tensor_scalar(low, act_b[:, :], 0.0, slope[:, 0:1], ALU.min, ALU.mult))
                        do(v.scalar_tensor_tensor(act_b[:, :], act_b[:, :], 0.0, low, ALU.max, ALU.add))
                        if plus is not None:
                            do(v.tensor_tensor(x_res[:, :], x_res[:, :], act_b[:, :], ALU.add))

        def hconv(weights_name, source, bias, plus=None):
            load_weights(weights_name, False)
            linear([source], act_b, to_table=True)
            sum_pass(True, False)
            by_degree(deg_d)
            sum_pass(False, False)
            by_degree(deg_s, bias, plus)

        def store_out():
            with phase("stored") as (block, m):
                @block.sync
                def _(sp):
                    full = (BLOCKS - 1) * P
                    sp.dma_start(out[0:full, :].rearrange("(b p) f -> p b f", p=P), blocks(x_res)[:, 0:BLOCKS - 1, :]).then_inc(m["stored"], 16)
                    sp.dma_start(out[full:NODES, :], x_res[0:NODES - full, (BLOCKS - 1) * F:]).then_inc(m["stored"], 16)
                    sp.wait_ge(m["stored"], 32)

        setup()
        split_keys()
        count()
        sort_by_src()
        walk_tables(True)
        segment_masks()

        layernorm(x_res, act_a)
        load_weights("L0_gnn_Wp1", True)
        linear([act_a], act_b, bias="L0_gnn_bp1", relu=True, to_table=True, send=3)
        max_pass()
        load_weights("L0_gnn_Wm1", True)
        linear([act_a, agg], act_b, bias="L0_gnn_bm1", relu=True, to_table=True, send=5)
        max_pass()
        load_weights("L0_gnn_Wm2", True)
        linear([act_b, agg], act_a, bias="L0_gnn_bm2", plus=act_b, send=5)
        layernorm(act_a, act_a, affine=("L0_gnn_ln2_g", "L0_gnn_ln2_b"))
        store_table(act_a)
        max_pass()
        load_weights("L0_gnn_Wm3", True)
        linear([act_a, agg], act_b, bias="L0_gnn_bm3", plus=act_a, send=5)
        layernorm(act_b, act_b, affine=("L0_gnn_ln3_g", "L0_gnn_ln3_b"), add_to=x_res)

        layernorm(x_res, act_a)
        load_weights("L1_gnn_W", False)
        linear([act_a], act_b, to_table=True)
        att = io["L1_gnn_att"]
        attention(True, att[0:1, :, 0:C], att[0:1, :, C:2 * C], send=11)
        attention_out(True, "L1_gnn_b", True)

        layernorm(x_res, act_a)
        for n in ("0", "1"):
            load_weights("L2_gnn_W" + n, False)
            linear([act_a], act_b, to_table=True)
            attention(False, *(io["L2_gnn_a_" + k + n].rearrange("(o h) c -> o h c", o=1) for k in ("src", "dst")), send=10)
            attention_out(False, "L2_gnn_b" + n, n == "1")

        assert sent_tiles[0] == TILES
        walk_tables(False)
        layernorm(x_res, act_a)
        hconv("L3_gnn_W1", act_a, "L3_gnn_b1")
        hconv("L3_gnn_W2", act_b, "L3_gnn_b2", plus=act_a)
        store_out()


INPUTS = ["x", "src", "dst", "L0_gnn_Wp1", "L0_gnn_bp1", "L0_gnn_Wm1", "L0_gnn_bm1", "L0_gnn_Wm2", "L0_gnn_bm2",
          "L0_gnn_Wm3", "L0_gnn_bm3", "L0_gnn_ln2_g", "L0_gnn_ln2_b", "L0_gnn_ln3_g", "L0_gnn_ln3_b",
          "L1_gnn_W", "L1_gnn_att", "L1_gnn_b", "L2_gnn_W0", "L2_gnn_a_src0", "L2_gnn_a_dst0", "L2_gnn_b0",
          "L2_gnn_W1", "L2_gnn_a_src1", "L2_gnn_a_dst1", "L2_gnn_b1", "L3_gnn_W1", "L3_gnn_b1", "L3_gnn_W2",
          "L3_gnn_b2", "L3_gnn_a"]


def kernel(**inputs):
    import numpy as np
    import concourse.bacc as bacc
    from concourse.bass_utils import run_bass_kernel_spmd

    nc = bacc.Bacc("TRN2", target_bir_lowering=False, num_devices=1)
    arrays, io = {}, {}
    for name in INPUTS:
        a = np.ascontiguousarray(inputs[name])
        arrays["in_" + name] = a
        io[name] = nc.dram_tensor("in_" + name, a.shape, mybir.dt.from_np(a.dtype), kind="ExternalInput").ap()
    out = nc.dram_tensor("out", (NODES, F), F32, kind="ExternalOutput").ap()
    build(nc, io, out)
    result = run_bass_kernel_spmd(nc, [arrays], core_ids=[0])
    return result.results[0]["out"]
```
